# Optimizing a Trainium2 kernel written in Bass

```python
import numpy as np
import jax
import jax.numpy as jnp

def _softmax(x, axis=-1):
    return jax.nn.softmax(x, axis=axis)

def _gelu(x):
    return jax.nn.gelu(x, approximate=True)

def _silu(x):
    return jax.nn.silu(x)

def _sigmoid(x):
    return jax.nn.sigmoid(x)

def _layernorm(x, axis=-1, eps=1e-05):
    m = jnp.mean(x, axis=axis, keepdims=True)
    v = jnp.var(x, axis=axis, keepdims=True)
    return (x - m) / jnp.sqrt(v + eps)

def _scatter_add(tgt, idx, src, axis=0):
    return tgt.at[idx].add(src)

def _segment_sum(src, seg, n):
    return jax.ops.segment_sum(src, seg, n)
kernel_name = 'mk_seq_preln_d1_jaxref_r8_48a0a1'

def setup_inputs(seed: int=0):
    np.random.seed(seed)
    _w = jnp.asarray

    def _L0_attn_setup():
        import jax, jax.numpy as jnp
        import numpy as np
        D = 128
        H = 16
        HD = D // H
        B = 2
        T = 256

        def _apply_rotary(x, rope):
            x1, x2 = (x[..., ::2], x[..., 1::2])
            sin, cos = (rope[..., ::2], rope[..., 1::2])
            return jnp.concatenate([x1 * cos - x2 * sin, x1 * sin + x2 * cos], axis=-1)
        key = jax.random.key(seed)
        k0, k1, k2 = jax.random.split(key, 3)
        s = 1.0 / np.sqrt(D)
        return {'x': jax.random.normal(k0, (B, T, D), dtype=jnp.float32), 'qkv_w': jax.random.normal(k1, (D, 3 * D), dtype=jnp.float32) * s, 'qkv_b': jnp.zeros((3 * D,), dtype=jnp.float32), 'out_w': jax.random.normal(k2, (D, D), dtype=jnp.float32) * s, 'out_b': jnp.zeros((D,), dtype=jnp.float32)}
    _L0_attn_in = _L0_attn_setup()

    def _L0_ffn_setup():
        import jax, jax.numpy as jnp
        import numpy as np
        B, N, D = (4, 256, 128)
        SPARSITY = 0.01
        key = jax.random.key(seed)
        k1, k2, k3 = jax.random.split(key, 3)
        x = jax.random.normal(k1, (B, N, D), dtype=jnp.float32)
        spatial = jax.random.normal(k2, (D, D), dtype=jnp.float32) * 0.02
        freq = jnp.fft.fft(spatial, axis=-1)
        k = int(D * SPARSITY)
        mag = jnp.abs(freq)
        kth = jax.lax.top_k(mag, k)[0][:, -1:]
        w_sparse = jnp.where(mag >= kth, freq, 0.0 + 0j)
        bias = jax.random.normal(k3, (D,), dtype=jnp.float32) * 0.01
        return {'x': x, 'w_freq_real': jnp.real(w_sparse).astype(jnp.float32), 'w_freq_imag': jnp.imag(w_sparse).astype(jnp.float32), 'bias': bias}
    _L0_ffn_in = _L0_ffn_setup()
    _d = {'L0_attn_x': _L0_attn_in['x'], 'L0_attn_qkv_w': _L0_attn_in['qkv_w'], 'L0_attn_qkv_b': _L0_attn_in['qkv_b'], 'L0_attn_out_w': _L0_attn_in['out_w'], 'L0_attn_out_b': _L0_attn_in['out_b'], 'L0_ffn_w_freq_real': _L0_ffn_in['w_freq_real'], 'L0_ffn_w_freq_imag': _L0_ffn_in['w_freq_imag'], 'L0_ffn_bias': _L0_ffn_in['bias']}
    _x0 = _d['L0_attn_x']
    _d['L0_attn_x'] = jax.random.normal(jax.random.fold_in(jax.random.key(seed), 1), (4, 1024, 128), dtype=_x0.dtype)
    del _x0
    return _d

def reference(L0_attn_x, L0_attn_qkv_w, L0_attn_qkv_b, L0_attn_out_w, L0_attn_out_b, L0_ffn_w_freq_real, L0_ffn_w_freq_imag, L0_ffn_bias):

    def _L0_attn_ref(x, qkv_w, qkv_b, out_w, out_b):
        import jax, jax.numpy as jnp
        import numpy as np
        D = 128
        H = 16
        HD = D // H
        B = 2
        T = 256

        def _apply_rotary(x, rope):
            x1, x2 = (x[..., ::2], x[..., 1::2])
            sin, cos = (rope[..., ::2], rope[..., 1::2])
            return jnp.concatenate([x1 * cos - x2 * sin, x1 * sin + x2 * cos], axis=-1)
        Bx, Tx, Dm = x.shape
        qkv = (x @ qkv_w + qkv_b).reshape(Bx, Tx, 3, H, HD).transpose(2, 0, 3, 1, 4)
        q, k, v = (qkv[0], qkv[1], qkv[2])
        inv_freq = 1.0 / 10000.0 ** (jnp.arange(0, HD, 2, dtype=jnp.float32) / HD)
        t = jnp.arange(Tx, dtype=jnp.float32)
        freqs = t[:, None] * inv_freq[None, :]
        rope = jnp.concatenate([jnp.sin(freqs), jnp.cos(freqs)], axis=-1)
        q = _apply_rotary(q, rope)
        k = _apply_rotary(k, rope)
        scale = HD ** (-0.5)
        scores = jnp.einsum('bhqd,bhkd->bhqk', q, k) * scale
        causal_mask = jnp.triu(jnp.ones((Tx, Tx), dtype=bool), 1)
        scores = jnp.where(causal_mask, -jnp.inf, scores)
        attn = jax.nn.softmax(scores, axis=-1)
        out = jnp.einsum('bhqk,bhkd->bhqd', attn, v)
        out = out.transpose(0, 2, 1, 3).reshape(Bx, Tx, Dm)
        return out @ out_w + out_b

    def _L0_ffn_ref(x, w_freq_real, w_freq_imag, bias):
        import jax, jax.numpy as jnp
        import numpy as np
        B, N, D = (4, 256, 128)
        SPARSITY = 0.01
        w = jax.lax.complex(w_freq_real, w_freq_imag)
        x_freq = jnp.fft.fft(x, axis=-1)
        y_freq = jnp.einsum('bnd,do->bno', x_freq, w)
        y = jnp.real(jnp.fft.ifft(y_freq, axis=-1))
        return y + bias
    x = L0_attn_x
    x = x + _L0_attn_ref(_layernorm(x, axis=-1), L0_attn_qkv_w, L0_attn_qkv_b, L0_attn_out_w, L0_attn_out_b)
    x = x + _L0_ffn_ref(_layernorm(x, axis=-1), L0_ffn_w_freq_real, L0_ffn_w_freq_imag, L0_ffn_bias)
    return x

_drawn_inputs = setup_inputs


def setup_inputs(seed=0):
    import zlib

    import numpy as np

    out = dict(_drawn_inputs(seed))
    spreads = {'L0_attn_qkv_b': (0.0, 0.1), 'L0_attn_out_b': (0.0, 0.1)}
    factors = {'L0_ffn_bias': 6.33}
    for name, (base, spread) in spreads.items():
        noise = np.random.default_rng([zlib.crc32(name.encode()), seed]).standard_normal(out[name].shape)
        drawn = base * np.exp(spread * noise) if base else spread * noise
        out[name] = jnp.asarray(drawn.astype(out[name].dtype))
    for name, factor in factors.items():
        out[name] = (out[name] * factor).astype(out[name].dtype)
    return out
```

```python
from contextlib import ExitStack

import concourse.bass as bass
from concourse import mybir

F32 = mybir.dt.float32
BF16 = mybir.dt.bfloat16
ACT = mybir.ActivationFunctionType
ALU = mybir.AluOpType
AX_X = mybir.AxisListType.X

P = 128
B, T, D = 4, 1024, 128
H, HD = 16, 8
HPG = 4
HG = H // HPG
G = B * HG
TILES = T // P
HALF = 512
HT = HALF // P
PARTS = 3
PR = PARTS * HD
KROWS = PARTS * PR
MROW = 96
SROWS = MROW + PARTS
VC = HD + 1
EPS = 1e-5
SCALE = float(HD) ** -0.5
NEG = -1e38

STEPS = []
for half in range(2):
    for kt in range(HT * (half + 1)):
        c0 = max(0, kt - HT * half) * P
        STEPS.append((half, kt, c0, HALF - c0, kt >= HT * half))
NS = len(STEPS)
UNITS = []
for s, (_, _, _, w, _) in enumerate(STEPS):
    UNITS += [(s, 0, 4)] if 2 * w <= HALF else [(s, 0, 2), (s, 2, 2)]
NU = len(UNITS)
UNITS_OF = [[n for n, u in enumerate(UNITS) if u[0] == s] for s in range(NS)]
DIAG = [n for n, u in enumerate(UNITS) if STEPS[u[0]][4]]
ND = len(DIAG)
LEAD = 2
RING = 8
HALF_END = [HT - 1, NS - 1]
assert NU % 2 == 0 and 2 * NU % RING == 0

MUNITS = []
for qt in range(HT):
    w = (qt + 1) * P
    n = HALF // w
    n = 4 if n >= 4 else 2 if n >= 2 else 1
    MUNITS += [(0, qt, h, n, 0, w, True, 0) for h in range(0, HPG, n)]
for qt in range(HT):
    w = (qt + 1) * P
    n = HALF // w
    n = 4 if n >= 4 else 2 if n >= 2 else 1
    MUNITS += [(1, qt, h, 1, 0, HALF, False, 0) for h in range(HPG)]
    MUNITS += [(1, qt, h, n, HALF, w, True, 1) for h in range(0, HPG, n)]
NM = len(MUNITS)
M_END = [sum(1 for m in MUNITS if m[0] == 0), NM]
assert NM % 2 == 0
M_AT = [round(NM * s / (NS - 1)) for s in range(NS)] + [NM]
M_T0 = 6
A_T0 = 5
assert M_AT[M_T0 - 1] >= M_END[0]
MISC = 4


def build(nc, x, w_qkv, b_qk, b_v, w_out, b_out, w_re, w_im, b_ffn,
          rope_c, rope_s, dft_c, dft_s, dft_ns, ident_in, identb_in, mask_in, q_scr, k_scr, out):
    with ExitStack() as ctx:
        def sb(name, shape, dt=F32):
            return ctx.enter_context(nc.sbuf_tensor(name, shape, dt))

        def sem(name):
            return ctx.enter_context(nc.semaphore(name))

        wq = sb("wq", [P, 5, P])
        bq = sb("bq", [P, 4])
        bv = sb("bv", [P, D])
        wo = sb("wo", [P, D])
        bo = sb("bo", [P, D])
        bf = sb("bf", [P, D])
        wr = sb("wr", [P, D])
        wi = sb("wi", [P, D])
        tc = sb("tc", [P, T])
        ts = sb("ts", [P, T])
        dc = sb("dc", [P, D])
        dsn = sb("dsn", [P, D])
        dns = sb("dns", [P, D])
        ident = sb("ident", [P, P])
        identb = sb("identb", [P, P], BF16)
        mask = sb("mask", [P, P], BF16)
        a12 = sb("a12", [P, 2, D])
        mffn = sb("mffn", [P, D])
        xs = sb("xs", [P, B * TILES, D])
        attn = sb("attn", [P, G, TILES, HPG * HD])
        vres = sb("vres", [P, G, TILES * HPG * VC])
        st = sb("st", [P, TILES, 6])
        mv = sb("mv", [P, B * TILES, 2])
        rstd = sb("rstd", [P, B * TILES])
        xn = sb("xn", [P, 2, HT, D])
        xnT = sb("xnT", [P, 2, HALF])
        prod = sb("prod", [P, 2, 2, HALF])
        rest = sb("rest", [P, 2, HALF])
        parts = sb("parts", [P, 2, 2, PARTS, HALF], BF16)
        qb = sb("qb", [P, 2, 2, HPG, HALF], BF16)
        kb = sb("kb", [P, 2, 2, HPG, HALF], BF16)
        vpad = sb("vpad", [P, 2, TILES, HPG, 32])
        pr = sb("pr", [P, RING, 2, HALF])
        oraw = sb("oraw", [P, 2, HALF])
        mpart = sb("mpart", [P, 2, 2, HPG, HT])
        negm = sb("negm", [P, 2, HPG * HT])
        mrest = sb("mrest", [P, 2, HPG * HT])
        mcut = sb("mcut", [P, 2, P], BF16)
        mT = sb("mT", [PARTS * HPG * HT, 2, P], BF16)
        rden = sb("rden", [P, 2, HT, HPG])
        at = sb("at", [P, TILES, D])
        aT = sb("aT", [P, T])
        st3 = sb("st3", [P, TILES, 6])
        mv3 = sb("mv3", [P, TILES, 2])
        rs3 = sb("rs3", [P, TILES])
        yr = sb("yr", [P, TILES, D])
        yn = sb("yn", [P, TILES, D])
        ynT = sb("ynT", [P, T])
        res = sb("res", [P, 2, HT, D])

        ps = ctx.enter_context(nc.psum_tensor("ps", [P, 8, HALF], F32))
        psb = ps[:, 7, :].bitcast(BF16)

        S_BANK = [0, 2]
        M_BANK = [4, 5]
        PV_BANK, MISC_BANK = 6, 7

        x_in = sem("x_in")
        consts_in = sem("consts_in")
        zeroed = sem("zeroed")
        ffn_a = sem("ffn_a")
        ffn_a_out = sem("ffn_a_out")
        ffn_m = sem("ffn_m")
        ffn_m_out = sem("ffn_m_out")
        dve_step = sem("dve_step")
        pool_step = sem("pool_step")
        var_done = sem("var_done")
        std_done = sem("std_done")
        xn_done = sem("xn_done")
        xnT_turned = sem("xnT_turned")
        xnT_done = sem("xnT_done")
        proj_done = sem("proj_done")
        proj_read = sem("proj_read")
        rot_done = sem("rot_done")
        part0_done = sem("part0_done")
        rest_done = sem("rest_done")
        part2_done = sem("part2_done")
        parts_out = [sem("parts_out0"), sem("parts_out1")]
        x_biased = sem("x_biased")
        q_in = [[sem(f"q_in{u}{h}") for h in range(2)] for u in range(2)]
        k_in = [[sem(f"k_in{u}{h}") for h in range(2)] for u in range(2)]
        m_in = [sem("m_in0"), sem("m_in1")]
        mscores_done = sem("mscores_done")
        max_done = sem("max_done")
        max_joined = sem("max_joined")
        mcut_done = sem("mcut_done")
        turned = sem("turned")
        misc_read = sem("misc_read")
        scores_done = sem("scores_done")
        exp_done = sem("exp_done")
        diag_done = sem("diag_done")
        v_ready = sem("v_ready")
        pv_done = sem("pv_done")
        oraw_done = sem("oraw_done")
        at_done = sem("at_done")
        t3_turned = sem("t3_turned")
        t3_out = sem("t3_out")
        mm3_done = sem("mm3_done")
        mm3_read = sem("mm3_read")
        var3_done = sem("var3_done")
        std3_done = sem("std3_done")
        yn_done = sem("yn_done")
        y_biased = sem("y_biased")
        res_done = sem("res_done")
        stored = [sem("stored0"), sem("stored1")]
        pool_gate = sem("pool_gate")
        dve_gate = sem("dve_gate")

        NCONST = 16
        x_v = x.rearrange("b (t p) d -> p b t d", p=P)
        o_v = out.rearrange("b (t p) d -> p b t d", p=P)

        block = ctx.enter_context(nc.Block())

        @block.sync
        def _(sp):
            for half in range(2):
                sp.sem_inc(parts_out[half], 16)
                sp.sem_inc(stored[half], 16)
            sp.dma_start(xs[:, 0:TILES, :], x_v[:, 0]).then_inc(x_in, 16)
            for dst, src in ((wq[:], w_qkv), (bq[:], b_qk), (bv[:], b_v.to_broadcast([P, D])),
                             (ident[:], ident_in), (tc[:], rope_c), (ts[:], rope_s),
                             (dc[:], dft_c), (dsn[:], dft_s), (dns[:], dft_ns), (wr[:], w_re), (wi[:], w_im),
                             (bf[:], b_ffn.to_broadcast([P, D])), (bo[:], b_out.to_broadcast([P, D])),
                             (wo[:], w_out), (identb[:], identb_in), (mask[:], mask_in)):
                sp.dma_start(dst, src).then_inc(consts_in, 16)
            for b in range(1, B):
                sp.wait_ge(x_in, 16 * b)
                sp.dma_start(xs[:, b * TILES:(b + 1) * TILES, :], x_v[:, b]).then_inc(x_in, 16)

            with sp.Fori(0, B) as b:
                for half in range(2):
                    for qk, scr in ((0, q_scr), (1, k_scr)):
                        sp.wait_ge(part2_done, 4 * b + 2 * half + qk + 1)
                        for part in range(PARTS):
                            dst = scr[bass.ds(b, 1), :, half, part].rearrange("o g r t -> (o g) r t")
                            src = parts[:, half, qk, part, :]
                            sp.dma_start(dst, src).then_inc(parts_out[half], 16)
            for half in range(2):
                sp.wait_ge(parts_out[half], 16 * 2 * PARTS * B + 16)

            q_rows = q_scr.rearrange("b g h a (d e) t -> (b g) h (a d) (e t)", d=HD)
            k_rows = k_scr.rearrange("b g h a (d e) t -> (b g) h (a d) (e t)", d=HD)

            def load_q(g, u, half):
                for rep in range(PARTS):
                    dst = qb[rep * PR:(rep + 1) * PR, u, half].rearrange("r e t -> r (e t)")
                    src = q_rows[g, half] if isinstance(g, int) else \
                        q_rows[bass.ds(g, 1), half].rearrange("o r t -> (o r) t")
                    sp.dma_start(dst, src).then_inc(q_in[u][half], 16)

            def load_k(g, u, half):
                rows = k_rows[g, half] if isinstance(g, int) else \
                    k_rows[bass.ds(g, 1), half].rearrange("o r t -> (o r) t")
                for rep in range(PARTS):
                    cut = PR - rep * HD
                    base = rep * PR
                    whole = kb[:, u, half].rearrange("r e t -> r (e t)")
                    sp.dma_start(whole[base:base + cut], rows[rep * HD:PR]).then_inc(k_in[u][half], 16)
                    if rep:
                        sp.dma_start(whole[base + cut:base + PR], rows[0:rep * HD]).then_inc(k_in[u][half], 16)

            sp.wait_ge(zeroed, 2)
            for u in range(2):
                for half in range(2):
                    load_q(u, u, half)
                    load_k(u, u, half)

            def max_rows(g, u, half):
                sp.wait_ge(misc_read, MISC * g + (0 if half == 0 else 1) + MREAD[half])
                dst = qb[MROW:MROW + PARTS, u, half].rearrange("r e (a q) -> r (e a) q", q=P)
                src = mT[:, half, :]
                sp.dma_start(dst, src).then_inc(m_in[half], 16)

            MREAD = [0, 0]

            def max_rows_to(count, u, half):
                sp.wait_ge(misc_read, count)
                dst = qb[MROW:MROW + PARTS, u, half].rearrange("r e (a q) -> r (e a) q", q=P)
                sp.dma_start(dst, mT[:, half, :]).then_inc(m_in[half], 16)

            max_rows_to(1, 0, 0)
            max_rows_to(2, 0, 1)

            def sp_group(i, u, last):
                g = i * 2 + u
                first = 2 + MISC * u
                if not last:
                    sp.wait_ge(scores_done, i * (2 * NU) + NU * u + UNITS_OF[HT - 1][-1] + 1)
                    load_q(g + 2, u, 0)
                if not (last and u == 1):
                    max_rows_to(i * (2 * MISC) + first + 2, 1 - u, 0)
                if not last:
                    sp.wait_ge(scores_done, i * (2 * NU) + NU * u + UNITS_OF[2 * HT - 1][-1] + 1)
                    load_k(g + 2, u, 0)
                if not (last and u == 1):
                    max_rows_to(i * (2 * MISC) + first + 3, 1 - u, 1)
                if not last:
                    sp.wait_ge(scores_done, i * (2 * NU) + NU * (u + 1))
                    load_q(g + 2, u, 1)
                    load_k(g + 2, u, 1)

            with sp.Fori(0, G // 2 - 1) as i:
                for u in range(2):
                    sp_group(i, u, False)
            for u in range(2):
                sp_group(G // 2 - 1, u, True)

            with sp.Fori(0, B) as b:
                for half in range(2):
                    sp.wait_ge(res_done, 2 * b + half + 1)
                    dst = o_v[:, bass.ds(b, 1), half * HT:(half + 1) * HT, :].rearrange("p o t d -> p (o t) d")
                    sp.dma_start(dst, res[:, half]).then_inc(stored[half], 16)
            for half in range(2):
                sp.wait_ge(stored[half], 16 * B + 16)

        @block.gpsimd
        def _(pool):
            pool.memset(qb[:].bitcast(F32), 0.0)
            pool.memset(vres[:], 1.0)
            pool.memset(vpad[:], 0.0)
            pool.memset(mcut[:].bitcast(F32), 0.0).then_inc(zeroed, 1)

            with pool.Fori(0, B) as b:
                for half in range(2):
                    k = 2 * b + half
                    for qk in range(2):
                        pool.wait_ge(proj_read, 5 * k + 2 * qk + 2)
                        pool.tensor_tensor(prod[:, qk, 0, :], prod[:, qk, 0, :], prod[:, qk, 1, :],
                                           ALU.add).then_inc(rot_done, 1)
                    for qk in range(2):
                        pool.wait_ge(part0_done, 2 * k + qk + 1)
                        pool.tensor_tensor(rest[:, qk, :], prod[:, qk, 0, :], parts[:, half, qk, 0, :],
                                           ALU.subtract).then_inc(rest_done, 1)

            chain = [0]

            def done(ins):
                chain[0] += 1
                ins.then_inc(pool_step, 1)
                return chain[0]

            def cut_max(before, half, max_count):
                at0 = chain[0]

                def own(ins):
                    n = done(ins) - at0
                    pool.wait_ge(pool_step, before + n)
                pool.wait_ge((max_done, max_joined)[half], max_count)
                m = negm[:, half, :]
                if half == 0:
                    src = mpart[:, 0, 0].rearrange("p e q -> p (e q)")
                else:
                    src = m
                n = HPG * HT
                pool.sem_inc(pool_gate)
                cut = [mcut[:, half, a * n:(a + 1) * n] for a in range(PARTS)]
                own(pool.tensor_copy(cut[0], src))
                own(pool.tensor_tensor(mrest[:, half, :], src, cut[0], ALU.subtract))
                pool.sem_inc(pool_gate)
                own(pool.tensor_copy(cut[1], mrest[:, half, :]))
                pool.tensor_tensor(cut[2], mrest[:, half, :], cut[1], ALU.subtract).then_inc(mcut_done, 1)

            def copy_v(g, u):
                pool.sem_inc(pool_gate)
                src = vres[:, g, :] if isinstance(g, int) else vres[:, bass.ds(g, 1), :].rearrange("p o f -> p (o f)")
                pool.tensor_copy(vpad[:, u, :, :, 0:VC].rearrange("p t e c -> p (t e) c"),
                                 src.rearrange("p (n c) -> p n c", c=VC)).then_inc(v_ready, 1)

            def diagonal(i, u, s):
                for n in UNITS_OF[s]:
                    _, _, heads = UNITS[n]
                    w = STEPS[s][3]
                    pool.wait_ge(exp_done, i * (2 * NU) + NU * u + n + 1)
                    pool.sem_inc(pool_gate)
                    at_slot = pr[:, (NU * u + n) % RING]
                    if heads == 2:
                        view, pat = at_slot[:, :, 0:P], [[0, 2], [1, P]]
                    else:
                        view = at_slot[:, :, 0:2 * w].rearrange("p a (c q) -> p a c q", c=2)[:, :, :, 0:P]
                        pat = [[0, 2], [0, 2], [1, P]]
                    pool.affine_select(out=view, in_=view, compare_op=ALU.is_ge, fill=0.0, base=0,
                                       pattern=pat, channel_multiplier=-1).then_inc(diag_done, 1)

            pool.wait_ge(proj_read, 5 * 2 * B)
            copy_v(0, 0)
            cut_max(0, 0, M_END[0])
            cut_max(3, 1, 1)

            def pool_group(i, u, last):
                g = i * 2 + u
                end = last and u == 1
                for s in range(0, HT):
                    diagonal(i, u, s)
                if not end:
                    cut_max(i * (2 * 6) + 6 + 6 * u, 0, i * (2 * NM) + NM * (u + 1) + M_END[0])
                    pool.wait_ge(pv_done, i * (2 * NS) + NS * u + NS)
                    copy_v(g + 1, 1 - u)
                for s in range(2 * HT, NS):
                    diagonal(i, u, s)
                if not end:
                    cut_max(i * (2 * 6) + 9 + 6 * u, 1, i * 2 + u + 2)

            with pool.Fori(0, G // 2 - 1) as i:
                for u in range(2):
                    pool_group(i, u, False)
                    if u == 0:
                        pass
            for u in range(2):
                pool_group(G // 2 - 1, u, True)

        @block.tensor
        def _(pe):
            pe.sem_inc(pv_done, NS)
            pe.sem_inc(oraw_done, 2)
            pe.wait_ge(consts_in, 16 * NCONST)
            pe.matmul(ps[:, 0, 0:D], wr[:], dc[:], start=True, stop=False)
            pe.matmul(ps[:, 0, 0:D], wi[:], dsn[:], start=False, stop=True)
            pe.matmul(ps[:, 1, 0:D], wi[:], dc[:], start=True, stop=False)
            pe.matmul(ps[:, 1, 0:D], wr[:], dns[:], start=False, stop=True).then_inc(ffn_a, 1)
            pe.wait_ge(ffn_a_out, 1)
            pe.matmul(ps[:, 2, 0:D], a12[:, 0, :], dc[:], start=True, stop=False)
            pe.matmul(ps[:, 2, 0:D], a12[:, 1, :], dns[:], start=False, stop=True).then_inc(ffn_m, 1)
            pe.wait_ge(ffn_m_out, 1)

            with pe.Fori(0, B) as b:
                for half in range(2):
                    k = 2 * b + half
                    pe.wait_ge(xn_done, k + 1)
                    for t in range(HT):
                        mm = pe.transpose(ps[:, 6 + half, t * P:(t + 1) * P], xn[:, half, t, :], ident[:])
                    mm.then_inc(xnT_turned, 1)
                for half in range(2):
                    k = 2 * b + half
                    pe.wait_ge(xnT_done, k + 1)
                    if half:
                        pe.wait_ge(proj_read, 5 * k)
                    for j in range(4):
                        pe.matmul(ps[:, 1 + j, :], wq[:, j, :], xnT[:, half, :],
                                  start=True, stop=True).then_inc(proj_done, 1)
                    for t in range(HT):
                        mm = pe.matmul(ps[:, 5, t * P:(t + 1) * P], xnT[:, half, t * P:(t + 1) * P], wq[:, 4, :],
                                       start=(t == 0), stop=True, skip_group_check=True)
                    mm.then_inc(proj_done, 1)
                    if not half:
                        continue
                pe.wait_ge(proj_read, 5 * (2 * b + 2))

            def max_scores(i, u, m):
                half, qt, h0, heads, k0, w, diag, _ = MUNITS[m]
                if isinstance(i, int) and i == 0 and u == 0 and m < 2:
                    pass
                else:
                    pe.wait_ge(max_done, i * (2 * NM) + NM * u + m - 1)
                bank = M_BANK[m % 2]
                for n in range(heads):
                    mm = pe.matmul(ps[:, bank, n * w:(n + 1) * w],
                                   qb[0:MROW, u, half, h0 + n, qt * P:(qt + 1) * P],
                                   kb[0:MROW, u, k0 // HALF, h0 + n, 0:w],
                                   start=(n == 0), stop=not diag, skip_group_check=True)
                if diag:
                    for n in range(heads):
                        mm = pe.matmul(ps[:, bank, (n + 1) * w - P:(n + 1) * w], identb[:], mask[:],
                                       start=False, stop=True, skip_group_check=True)
                mm.then_inc(mscores_done, 1)

            def wait_operands(i, u, half):
                pe.wait_ge(q_in[u][half], i * 48 + 48)
                pe.wait_ge(k_in[u][half], i * 80 + 80)

            def turn_max(uses, cuts, half):
                pe.wait_ge(mcut_done, cuts)
                if uses is not None:
                    pe.wait_ge(misc_read, uses)
                pe.transpose(psb[:, 0:P], mcut[:, half, :], identb[:]).then_inc(turned, 1)

            def scores(i, u, n):
                s, h0, heads = UNITS[n]
                half, kt, c0, w, _ = STEPS[s]
                if not (isinstance(i, int) and i == 0 and u == 0 and n < 2):
                    pe.wait_ge(exp_done, i * (2 * NU) + NU * u + n - 1)
                bank = S_BANK[n % 2]
                per = heads // 2
                for m in range(heads):
                    col = (m % per) * w
                    mm = pe.matmul(ps[:, bank + m // per, col:col + w],
                                   kb[0:SROWS, u, kt // HT, h0 + m, (kt % HT) * P:(kt % HT + 1) * P],
                                   qb[0:SROWS, u, half, h0 + m, c0:HALF],
                                   start=(m % per == 0), stop=True, skip_group_check=True)
                mm.then_inc(scores_done, 1)

            def value_step(i, u, s):
                half, kt, c0, w, diag = STEPS[s]
                n = UNITS_OF[s][-1]
                if diag:
                    pe.wait_ge(diag_done, i * (2 * ND) + ND * u + DIAG.index(n) + 1)
                else:
                    pe.wait_ge(exp_done, i * (2 * NU) + NU * u + n + 1)
                if kt == 0:
                    pe.wait_ge(oraw_done, i * 4 + 2 * u + half + 2)
                if s == 0:
                    pe.wait_ge(v_ready, i * 2 + u + 1)
                for e in range(HPG):
                    if len(UNITS_OF[s]) == 2:
                        slot, src = (NU * u + UNITS_OF[s][e // 2]) % RING, (e % 2, 0)
                    else:
                        slot, src = (NU * u + n) % RING, (e // 2, (e % 2) * w)
                    mm = pe.matmul(ps[32 * e:32 * e + 32, PV_BANK, c0:HALF], vpad[:, u, kt, e, :],
                                   pr[:, slot, src[0], src[1]:src[1] + w],
                                   start=(kt == 0), stop=(s in HALF_END), skip_group_check=True)
                mm.then_inc(pv_done, 1)

            def turn_out(i, u, half, uses):
                pe.wait_ge(oraw_done, i * 4 + 2 * u + half + 3)
                pe.wait_ge(misc_read, uses)
                for t in range(HT):
                    mm = pe.transpose(ps[:, MISC_BANK, t * P:(t + 1) * P], oraw[:, half, t * P:(t + 1) * P], ident[:])
                mm.then_inc(turned, 1)

            pe.wait_ge(zeroed, 2)
            for half in range(2):
                wait_operands(0, 0, half)
                for m in range(M_END[half - 1] if half else 0, M_END[half]):
                    max_scores(0, 0, m)
                turn_max([None, 1][half], half + 1, half)
            pe.wait_ge(m_in[0], 16)
            for s in range(LEAD):
                for n in UNITS_OF[s]:
                    scores(0, 0, n)

            def pe_group(i, u, last):
                end = last and u == 1
                nxt = (i, 1) if u == 0 else (i + 1, 0)
                uses = 2 + MISC * u
                for s in range(NS):
                    a = s + LEAD
                    if a < NS:
                        if a == HT:
                            pe.wait_ge(m_in[1], i * 32 + 16 * u + 16)
                        units = [(i, u, n) for n in UNITS_OF[a]]
                    elif not end:
                        if a == NS:
                            pe.wait_ge(m_in[0], i * 32 + 16 * u + 32)
                        units = [(*nxt, n) for n in UNITS_OF[a - NS]]
                    else:
                        units = []
                    if units:
                        scores(*units[0])
                    value_step(i, u, s)
                    for n in units[1:]:
                        scores(*n)
                    if not end:
                        for m in range(M_AT[s], M_AT[s + 1]):
                            if m == 0:
                                wait_operands(*nxt, 0)
                            if m == M_END[0]:
                                wait_operands(*nxt, 1)
                            max_scores(*nxt, m)
                    if s == A_T0:
                        turn_out(i, u, 0, i * (2 * MISC) + uses)
                    if s == M_T0 and not end:
                        turn_max(i * (2 * MISC) + uses + 1, i * 4 + 2 * u + 3, 0)
                    if s == NS - 1:
                        if not end:
                            turn_max(i * (2 * MISC) + uses + 2, i * 4 + 2 * u + 4, 1)
                        turn_out(i, u, 1, i * (2 * MISC) + uses + (1 if end else 3))

            with pe.Fori(0, G // 2 - 1) as i:
                for u in range(2):
                    pe_group(i, u, False)
            for u in range(2):
                pe_group(G // 2 - 1, u, True)

            pe.wait_ge(misc_read, 2 + MISC * G - 2)
            with pe.Fori(0, B) as b:
                for step in range(2):
                    src, turned_dst = ((at, aT), (yn, ynT))[step]
                    if step == 0:
                        pe.wait_ge(at_done, b + 1)
                    else:
                        pe.wait_ge(yn_done, b + 1)
                    for t in range(TILES):
                        mm = pe.transpose(ps[:, t // HT, (t % HT) * P:(t % HT + 1) * P], src[:, t, :], ident[:])
                    mm.then_inc(t3_turned, 1)
                    pe.wait_ge(t3_out, 2 * b + step + 1)
                    for t in range(TILES):
                        mm = pe.matmul(ps[:, 2 + t // HT, (t % HT) * P:(t % HT + 1) * P],
                                       turned_dst[:, t * P:(t + 1) * P], (wo, mffn)[step][:],
                                       start=(t % HT == 0), stop=True, skip_group_check=True)
                    mm.then_inc(mm3_done, 1)
                    if step == 0:
                        pe.wait_ge(mm3_read, b + 1)
                    else:
                        pe.wait_ge(res_done, 2 * b + 2)

        @block.scalar
        def _(act):
            act.wait_ge(ffn_a, 1)
            act.activation(a12[:], ps[:, 0:2, 0:D], ACT.Copy, scale=1.0 / D).then_inc(ffn_a_out, 1)
            act.wait_ge(ffn_m, 1)
            act.copy(mffn[:], ps[:, 2, 0:D]).then_inc(ffn_m_out, 1)
            act.wait_ge(var_done, 1)
            act.activation(rstd[:], rstd[:], ACT.Sqrt).then_inc(std_done, 1)
            with act.Fori(0, B) as b:
                for half in range(2):
                    act.wait_ge(xnT_turned, 2 * b + half + 1)
                    act.copy(xnT[:, half, :], ps[:, 6 + half, :]).then_inc(xnT_done, 1)

            def exp(i, u, n):
                s, _, heads = UNITS[n]
                w = STEPS[s][3]
                act.wait_ge(scores_done, i * (2 * NU) + NU * u + n + 1)
                behind = NU * u + n - RING
                if isinstance(i, int) and 2 * NU * i + behind < 0:
                    pass
                else:
                    step = NS * (behind // NU) + UNITS[behind % NU][0] + 1
                    act.wait_ge(pv_done, i * (2 * NS) + NS + step)
                wide = w * heads // 2
                act.activation(pr[:, (NU * u + n) % RING, :, 0:wide], ps[:, S_BANK[n % 2]:S_BANK[n % 2] + 2, 0:wide],
                               ACT.Exp, scale=SCALE).then_inc(exp_done, 1)

            for s in range(LEAD):
                for n in UNITS_OF[s]:
                    exp(0, 0, n)

            def act_group(i, u, last):
                end = last and u == 1
                nxt = (i, 1) if u == 0 else (i + 1, 0)
                for s in range(NS):
                    a = s + LEAD
                    if a < NS:
                        for n in UNITS_OF[a]:
                            exp(i, u, n)
                    elif not end:
                        for n in UNITS_OF[a - NS]:
                            exp(*nxt, n)
                    if s in HALF_END:
                        half = HALF_END.index(s)
                        act.wait_ge(pv_done, i * (2 * NS) + NS + NS * u + s + 1)
                        act.copy(oraw[:, half, :], ps[:, PV_BANK, :]).then_inc(oraw_done, 1)

            with act.Fori(0, G // 2 - 1) as i:
                for u in range(2):
                    act_group(i, u, False)
            for u in range(2):
                act_group(G // 2 - 1, u, True)

            with act.Fori(0, B) as b:
                act.wait_ge(t3_turned, 2 * b + 1)
                act.copy(aT[:].rearrange("p (a q) -> p a q", a=2), ps[:, 0:2, :]).then_inc(t3_out, 1)
                act.wait_ge(var3_done, b + 1)
                act.activation(rs3[:], rs3[:], ACT.Sqrt).then_inc(std3_done, 1)
                act.wait_ge(t3_turned, 2 * b + 2)
                act.copy(ynT[:].rearrange("p (a q) -> p a q", a=2), ps[:, 0:2, :]).then_inc(t3_out, 1)

        @block.vector
        def _(dve):
            def own(ins, count):
                ins.then_inc(dve_step, 1)
                dve.wait_ge(dve_step, count)

            dve.memset(kb[:, :, :, :, :].rearrange("p u h e t -> p (u h e t)").bitcast(F32), 0.0)
            own(dve.memset(mpart[:], 0.0), 1)
            dve.memset(kb[MROW:P].rearrange("p u h e t -> p (u h e t)"), 1.0).then_inc(zeroed, 1)

            for b in range(B):
                dve.wait_ge(x_in, 16 * b + 16)
                for t in range(TILES):
                    ins = dve.bn_stats(st[:, t, :], xs[:, b * TILES + t, :])
                own(ins, 2 * b + 2)
                for t in range(TILES):
                    ins = dve.bn_aggr(mv[:, b * TILES + t, :], st[:, t, :])
                own(ins, 2 * b + 3)
            n0 = 1 + 2 * B
            dve.tensor_scalar(rstd[:], mv[:, :, 1], EPS, None, ALU.add).then_inc(var_done, 1)
            dve.wait_ge(std_done, 1)
            own(dve.reciprocal(rstd[:], rstd[:]), n0 + 1)
            dve.wait_ge(consts_in, 16 * NCONST)

            with dve.Fori(0, B) as b:
                for half in range(2):
                    for t in range(HT):
                        j = b * TILES + half * HT + t
                        ins = dve.tensor_scalar(xn[:, half, t, :],
                                                xs[:, bass.ds(j, 1), :].rearrange("p o d -> p (o d)"),
                                                mv[:, bass.ds(j, 1), 0], rstd[:, bass.ds(j, 1)],
                                                ALU.subtract, ALU.mult)
                    ins.then_inc(xn_done, 1)
                for half in range(2):
                    k = 2 * b + half
                    dve.wait_ge(parts_out[half], b * (16 * 2 * PARTS) + 16)
                    for j in range(4):
                        dve.wait_ge(proj_done, 5 * k + j + 1)
                        dve.scalar_tensor_tensor(out=prod[:, j // 2, j % 2, :], in0=ps[:, 1 + j, :],
                                                 scalar=bq[:, j:j + 1],
                                                 in1=(tc, ts)[j % 2][:, half * HALF:(half + 1) * HALF],
                                                 op0=ALU.add, op1=ALU.mult).then_inc(proj_read, 1)
                    for qk in range(2):
                        dve.wait_ge(rot_done, 2 * k + qk + 1)
                        dve.tensor_copy(parts[:, half, qk, 0, :], prod[:, qk, 0, :]).then_inc(part0_done, 1)
                    dve.wait_ge(proj_done, 5 * k + 5)
                    for t in range(HT):
                        dst = vres[:, bass.ds(b * HG, HG), :].rearrange("p g (t e c) -> p g t e c", e=HPG, c=VC)[
                            :, :, half * HT + t, :, 0:HD]
                        ins = dve.tensor_tensor(dst, ps[:, 5, t * P:(t + 1) * P].rearrange("p (g e c) -> p g e c", e=HPG, c=HD),
                                                bv[:].rearrange("p (g e c) -> p g e c", e=HPG, c=HD), ALU.add)
                    ins.then_inc(proj_read, 1)
                    for qk in range(2):
                        dve.wait_ge(rest_done, 2 * k + qk + 1)
                        own(dve.tensor_copy(parts[:, half, qk, 1, :], rest[:, qk, :]),
                            4 * b + (n0 + 2 + 2 * half + qk))
                        dve.tensor_tensor(parts[:, half, qk, 2, :], rest[:, qk, :], parts[:, half, qk, 1, :],
                                          ALU.subtract).then_inc(part2_done, 1)
            n1 = n0 + 1 + 4 * B

            def take_max(i, u, m):
                half, qt, h0, heads, _, w, _, which = MUNITS[m]
                dve.wait_ge(mscores_done, i * (2 * NM) + NM * u + m + 1)
                dve.tensor_reduce(mpart[:, half, which, h0:h0 + heads, qt],
                                  ps[:, M_BANK[m % 2], 0:heads * w].rearrange("p (e k) -> p e k", e=heads),
                                  AX_X, ALU.max, negate=True).then_inc(max_done, 1)
                if m == NM - 1:
                    dve.wait_ge(max_done, i * (2 * NM) + NM * u + NM)
                    dve.tensor_tensor(negm[:, 1, :], mpart[:, 1, 0].rearrange("p e q -> p (e q)"),
                                      mpart[:, 1, 1].rearrange("p e q -> p (e q)"), ALU.min).then_inc(max_joined, 1)

            def max_row_out(i, count, half, rows):
                dve.wait_ge(turned, count)
                if rows is not None:
                    dve.wait_ge(m_in[half], rows)
                n = PARTS * HPG * HT
                dve.tensor_copy(mT[:, half, :], psb[0:n, 0:P]).then_inc(misc_read, 1)

            def outputs(i, u, half, count, own_count):
                dve.wait_ge(turned, count)
                o = ps[:, MISC_BANK, :].rearrange("p (t e c) -> p t e c", t=HT, c=32)
                own(dve.reciprocal(rden[:, half], o[:, :, :, HD]), own_count)
                g = i * 2 + u
                dst = attn[:, bass.ds(g, 1), half * HT:(half + 1) * HT, :] if not isinstance(g, int) else \
                    attn[:, g:g + 1, half * HT:(half + 1) * HT, :]
                dst = dst.rearrange("p o t (e c) -> p (o t) e c", c=HD)
                dve.tensor_tensor(dst, o[:, :, :, 0:HD],
                                  rden[:, half].rearrange("p t (e o) -> p t e o", o=1).to_broadcast([P, HT, HPG, HD]),
                                  ALU.mult).then_inc(misc_read, 1)

            for half in range(2):
                for m in range(M_END[half - 1] if half else 0, M_END[half]):
                    take_max(0, 0, m)
                max_row_out(0, half + 1, half, None)

            def dve_group(i, u, last):
                end = last and u == 1
                nxt = (i, 1) if u == 0 else (i + 1, 0)
                uses = 2 + MISC * u
                for s in range(NS):
                    if not end:
                        for m in range(M_AT[s], M_AT[s + 1]):
                            take_max(*nxt, m)
                    if s == A_T0:
                        outputs(i, u, 0, i * (2 * MISC) + uses + 1, i * 4 + n1 + 2 * u + 1)
                    if s == M_T0 and not end:
                        max_row_out(i, i * (2 * MISC) + uses + 2, 0, i * 32 + 16 * u + 16)
                    if s == NS - 1:
                        if not end:
                            max_row_out(i, i * (2 * MISC) + uses + 3, 1, i * 32 + 16 * u + 16)
                        outputs(i, u, 1, i * (2 * MISC) + uses + (2 if end else 4), i * 4 + n1 + 2 * u + 2)

            with dve.Fori(0, G // 2 - 1) as i:
                for u in range(2):
                    dve_group(i, u, False)
            for u in range(2):
                dve_group(G // 2 - 1, u, True)
            n2 = n1 + 2 * G

            def wide(row):
                return row[:].rearrange("p (o d) -> p o d", o=1).to_broadcast([P, TILES, D])

            with dve.Fori(0, B) as b:
                c = b * 5 + n2
                ins = dve.tensor_copy(at[:].rearrange("p t (g c) -> p g t c", g=HG), attn[:, bass.ds(b * HG, HG)])
                ins.then_inc(at_done, 1)
                dve.wait_ge(mm3_done, 2 * b + 1)
                for half in range(2):
                    ins = dve.tensor_tensor(yr[:, half * HT:(half + 1) * HT, :],
                                            xs[:, bass.ds(b * TILES + half * HT, HT), :],
                                            ps[:, 2 + half, :].rearrange("p (t d) -> p t d", d=D), ALU.add)
                ins.then_inc(mm3_read, 1)
                dve.wait_ge(mm3_read, b + 1)
                own(dve.tensor_tensor(yr[:], yr[:], wide(bo), ALU.add), c + 1)
                for t in range(TILES):
                    ins = dve.bn_stats(st3[:, t, :], yr[:, t, :])
                ins.then_inc(dve_step, 1)
                dve.wait_ge(dve_step, c + 2)
                dve.sem_inc(dve_gate)
                for t in range(TILES):
                    ins = dve.bn_aggr(mv3[:, t, :], st3[:, t, :])
                own(ins, c + 3)
                dve.tensor_scalar(rs3[:], mv3[:, :, 1], EPS, None, ALU.add).then_inc(var3_done, 1)
                dve.wait_ge(std3_done, b + 1)
                own(dve.reciprocal(rs3[:], rs3[:]), c + 4)
                for t in range(TILES):
                    ins = dve.tensor_scalar(yn[:, t, :], yr[:, t, :],
                                            mv3[:, t, 0:1], rs3[:, t:t + 1], ALU.subtract, ALU.mult)
                ins.then_inc(yn_done, 1)
                dve.wait_ge(yn_done, b + 1)
                own(dve.tensor_tensor(yr[:], yr[:], wide(bf), ALU.add), c + 5)
                dve.wait_ge(mm3_done, 2 * b + 2)
                for half in range(2):
                    dve.wait_ge(stored[half], 16 * b + 16)
                    ins = dve.tensor_tensor(res[:, half], yr[:, half * HT:(half + 1) * HT, :],
                                            ps[:, 2 + half, :].rearrange("p (t d) -> p t d", d=D), ALU.add)
                    ins.then_inc(res_done, 1)


def kernel(**inputs):
    import numpy as np
    import concourse.bacc as bacc
    from concourse.bass_utils import run_bass_kernel_spmd as run

    x = np.ascontiguousarray(inputs["L0_attn_x"])
    w = np.asarray(inputs["L0_attn_qkv_w"])
    bias = np.asarray(inputs["L0_attn_qkv_b"])

    g, d, e = np.meshgrid(np.arange(HG), np.arange(HD), np.arange(HPG), indexing="ij")
    even = 2 * (d % (HD // 2)) + d // (HD // 2)
    odd = 2 * (d % (HD // 2)) + 1 - d // (HD // 2)
    head = (g * HPG + e) * HD
    straight, swapped = (head + even).reshape(-1), (head + odd).reshape(-1)
    cols = [straight, swapped, D + straight, D + swapped]
    w_qkv = np.ascontiguousarray(np.stack([w[:, c] for c in cols] + [w[:, 2 * D:]], axis=1))
    b_qk = np.ascontiguousarray(np.stack([bias[c] for c in cols], axis=1))

    f = (np.float32(1.0) / np.float32(10000.0) ** (np.arange(0, HD, 2, dtype=np.float32) / np.float32(HD))).astype(np.float32)
    angle = (np.arange(T, dtype=np.float32)[:, None] * f[None, :]).astype(np.float64)
    rope = np.concatenate([np.sin(angle), np.cos(angle)], axis=-1)
    sin, cos = rope[:, 0::2], rope[:, 1::2]
    dim = d.reshape(-1)
    rope_c = np.ascontiguousarray(cos[:, dim % 4].T.astype(np.float32))
    rope_s = np.ascontiguousarray((sin[:, dim % 4] * np.where(dim < 4, -1.0, 1.0)).T.astype(np.float32))
    k = np.arange(D)
    turn = 2 * np.pi * (k[:, None] * k[None, :] % D) / D
    dft_c, dft_s = np.cos(turn).astype(np.float32), np.sin(turn).astype(np.float32)
    eye = np.eye(P, dtype=np.float32)
    bf = mybir.dt.np(BF16)
    future = np.where(np.arange(P)[None, :] > np.arange(P)[:, None], NEG, 0.0).astype(bf)

    nc = bacc.Bacc("TRN2", target_bir_lowering=False, num_devices=1)
    arrays, args = {}, []
    for name, a in (("x", x), ("w_qkv", w_qkv), ("b_qk", b_qk), ("b_v", bias[None, 2 * D:]),
                    ("w_out", inputs["L0_attn_out_w"]), ("b_out", np.asarray(inputs["L0_attn_out_b"])[None, :]),
                    ("w_re", inputs["L0_ffn_w_freq_real"]), ("w_im", inputs["L0_ffn_w_freq_imag"]),
                    ("b_ffn", np.asarray(inputs["L0_ffn_bias"])[None, :]),
                    ("rope_c", rope_c), ("rope_s", rope_s), ("dft_c", dft_c), ("dft_s", dft_s), ("dft_ns", -dft_s),
                    ("ident", eye), ("identb", eye.astype(bf)), ("mask", future)):
        a = np.ascontiguousarray(a)
        arrays[f"in_{name}"] = a
        args.append(nc.dram_tensor(f"in_{name}", a.shape, mybir.dt.from_np(a.dtype), kind="ExternalInput").ap())
    for name in ("q_scr", "k_scr"):
        args.append(nc.dram_tensor(name, (B, HG, 2, PARTS, HD * HPG, HALF), BF16, kind="Internal").ap())
    args.append(nc.dram_tensor("out_0", (B, T, D), F32, kind="ExternalOutput").ap())
    build(nc, *args)
    r = run(nc, [arrays], core_ids=[0])
    return r.results[0]["out_0"]
```

```python
from contextlib import ExitStack

import concourse.bass as bass
from concourse import mybir

F32 = mybir.dt.float32
BF16 = mybir.dt.bfloat16
ACT = mybir.ActivationFunctionType
ALU = mybir.AluOpType
AX_X = mybir.AxisListType.X

P = 128
B, T, D = 4, 1024, 128
H, HD = 16, 8
HPG = 4
HG = H // HPG
G = B * HG
TILES = T // P
HALF = 512
HT = HALF // P
PARTS = 3
PR = PARTS * HD
KROWS = PARTS * PR
MROW = 96
SROWS = MROW + PARTS
VC = HD + 1
EPS = 1e-5
SCALE = float(HD) ** -0.5
NEG = -1e38

STEPS = []
for half in range(2):
    for kt in range(HT * (half + 1)):
        c0 = max(0, kt - HT * half) * P
        STEPS.append((half, kt, c0, HALF - c0, kt >= HT * half))
NS = len(STEPS)
UNITS = []
for s, (_, _, _, w, _) in enumerate(STEPS):
    UNITS += [(s, 0, 4)] if 2 * w <= HALF else [(s, 0, 2), (s, 2, 2)]
NU = len(UNITS)
UNITS_OF = [[n for n, u in enumerate(UNITS) if u[0] == s] for s in range(NS)]
DIAG = [n for n, u in enumerate(UNITS) if STEPS[u[0]][4]]
ND = len(DIAG)
LEAD = 2
RING = 8
HALF_END = [HT - 1, NS - 1]
assert NU % 2 == 0 and 2 * NU % RING == 0

MUNITS = []
for qt in range(HT):
    w = (qt + 1) * P
    n = HALF // w
    n = 4 if n >= 4 else 2 if n >= 2 else 1
    MUNITS += [(0, qt, h, n, 0, w, True, 0) for h in range(0, HPG, n)]
for qt in range(HT):
    w = (qt + 1) * P
    n = HALF // w
    n = 4 if n >= 4 else 2 if n >= 2 else 1
    MUNITS += [(1, qt, h, 1, 0, HALF, False, 0) for h in range(HPG)]
    MUNITS += [(1, qt, h, n, HALF, w, True, 1) for h in range(0, HPG, n)]
NM = len(MUNITS)
M_END = [sum(1 for m in MUNITS if m[0] == 0), NM]
assert NM % 2 == 0
_cost = [m[3] * m[5] + P // 2 for m in MUNITS]
M_AT = [0]
for s in range(NS):
    share = sum(st[3] + HALF // 2 for st in STEPS[:s + 1]) / sum(st[3] + HALF // 2 for st in STEPS)
    M_AT.append(sum(1 for m in range(NM) if sum(_cost[:m + 1]) <= share * sum(_cost) + 1))
A_T0 = HT
M_T0 = HT + 1
assert M_AT[M_T0] >= M_END[0] and M_AT[NS] == NM
def _ring_order(last):
    order = []
    for s in range(NS):
        if not last:
            order += [("max", m) for m in range(M_AT[s], M_AT[s + 1])]
        order += [("turned maxima", 1)] * (s == 0) + [("turned outputs", 0)] * (s == A_T0)
        if not last:
            order += [("turned maxima", 0)] * (s == M_T0)
        order += [("turned outputs", 1)] * (s == NS - 1)
    return {use: n for n, use in enumerate(order)}


NRING = 3
AT_RING = _ring_order(False)
AT_RING_LAST = _ring_order(True)
RING_USES = len(AT_RING)
RING_FIRST = NM + 1
assert RING_USES % NRING == 0 and RING_FIRST % NRING == 0
FIRST_POS = {m: m if m < M_END[0] else m + 1 for m in range(NM)}


def build(nc, x, w_qkv, b_qk, b_v, w_out, b_out, w_re, w_im, b_ffn,
          rope_c, rope_s, dft_c, dft_s, dft_ns, ident_in, identb_in, mask_in, q_scr, k_scr, out):
    with ExitStack() as ctx:
        def sb(name, shape, dt=F32):
            return ctx.enter_context(nc.sbuf_tensor(name, shape, dt))

        def sem(name):
            return ctx.enter_context(nc.semaphore(name))

        wq = sb("wq", [P, 5, P])
        bq = sb("bq", [P, 4])
        bv = sb("bv", [P, D])
        wo = sb("wo", [P, D])
        bo = sb("bo", [P, D])
        bf = sb("bf", [P, D])
        wr = sb("wr", [P, D])
        wi = sb("wi", [P, D])
        tc = sb("tc", [P, T])
        ts = sb("ts", [P, T])
        dc = sb("dc", [P, D])
        dsn = sb("dsn", [P, D])
        dns = sb("dns", [P, D])
        ident = sb("ident", [P, P])
        identb = sb("identb", [P, P], BF16)
        mask = sb("mask", [P, P], BF16)
        a12 = sb("a12", [P, 2, D])
        mffn = sb("mffn", [P, D])
        xs = sb("xs", [P, B * TILES, D])
        attn = sb("attn", [P, G, TILES, HPG * HD])
        vres = sb("vres", [P, G, TILES * HPG * VC])
        st = sb("st", [P, TILES, 6])
        mv = sb("mv", [P, TILES, 2])
        rstd = sb("rstd", [P, TILES])
        xn = sb("xn", [P, 2, HT, D])
        xnT = sb("xnT", [P, 2, HALF])
        parts = sb("parts", [P, 2, 2, PARTS, HALF], BF16)
        qb = sb("qb", [P, 2, 2, HPG, HALF], BF16)
        kb = sb("kb", [P, 2, 2, HPG, HALF], BF16)
        vpad = sb("vpad", [P, 2, TILES, HPG, 32])
        pr = sb("pr", [P, RING, 2, HALF])
        oraw = sb("oraw", [P, 2, HALF])
        mpart = sb("mpart", [P, 2, 2, HPG, HT])
        negm = sb("negm", [P, 2, HPG * HT])
        mrest = sb("mrest", [P, 2, HPG * HT])
        mcut = sb("mcut", [P, 2, P], BF16)
        mT = sb("mT", [PARTS * HPG * HT, 2, P], BF16)
        rden = sb("rden", [P, 2, HT, HPG])
        st3 = sb("st3", [P, TILES, 6])
        mv3 = sb("mv3", [P, TILES, 2])
        mean3 = sb("mean3", [P, B * TILES])
        rs3 = sb("rs3", [P, B * TILES])

        prod = [[pr[:, 2 * half + qk] for qk in range(2)] for half in range(2)]
        rest = [[pr[:, 4 + half, qk, :] for qk in range(2)] for half in range(2)]
        at, aT, yn, ynT = ([pr[:, 2 * n + half, 0, :] for half in range(2)] for n in range(4))
        res = [pr[:, half, 1, :] for half in range(2)]

        ps = ctx.enter_context(nc.psum_tensor("ps", [P, 8, HALF], F32))

        S_BANK = [0, 2]
        PV_BANK = 6
        RING_BANK = [4, 5, 7]

        x_in = sem("x_in")
        consts_in = sem("consts_in")
        zeroed = sem("zeroed")
        ffn_a = sem("ffn_a")
        ffn_a_out = sem("ffn_a_out")
        ffn_m = sem("ffn_m")
        ffn_m_out = sem("ffn_m_out")
        dve_step = sem("dve_step")
        pool_step = sem("pool_step")
        var_done = sem("var_done")
        std_done = sem("std_done")
        xn_done = sem("xn_done")
        xnT_turned = sem("xnT_turned")
        xnT_done = sem("xnT_done")
        proj_done = sem("proj_done")
        proj_read = sem("proj_read")
        rot_done = sem("rot_done")
        part0_done = sem("part0_done")
        rest_done = sem("rest_done")
        part2_done = sem("part2_done")
        parts_out = [sem("parts_out0"), sem("parts_out1")]
        q_in = [[sem(f"q_in{u}{h}") for h in range(2)] for u in range(2)]
        k_in = [[sem(f"k_in{u}{h}") for h in range(2)] for u in range(2)]
        m_in = [sem("m_in0"), sem("m_in1")]
        ring_filled = sem("ring_filled")
        ring_read = sem("ring_read")
        max_joined = sem("max_joined")
        mcut_done = sem("mcut_done")
        scores_done = sem("scores_done")
        exp_done = sem("exp_done")
        diag_done = sem("diag_done")
        v_ready = sem("v_ready")
        pv_done = sem("pv_done")
        oraw_done = sem("oraw_done")
        at_done = sem("at_done")
        a_turned = sem("a_turned")
        aT_done = sem("aT_done")
        out_proj_done = sem("out_proj_done")
        out_proj_read = sem("out_proj_read")
        var3_done = sem("var3_done")
        std3_done = sem("std3_done")
        yn_done = sem("yn_done")
        y_turned = sem("y_turned")
        ynT_done = sem("ynT_done")
        ffn_done = sem("ffn_done")
        ffn_read = sem("ffn_read")
        res_done = sem("res_done")
        stored = [sem("stored0"), sem("stored1")]
        part1_done = sem("part1_done")
        late_in = sem("late_in")
        act_gate = sem("act_gate")
        pool_gate = sem("pool_gate")
        dve_gate = sem("dve_gate")

        EARLY, LATE = 6, 10
        x_v = x.rearrange("b (t p) d -> p b t d", p=P)
        o_v = out.rearrange("b (t p) d -> p b t d", p=P)

        block = ctx.enter_context(nc.Block())

        @block.sync
        def _(sp):
            for half in range(2):
                sp.sem_inc(parts_out[half], 16)
                sp.sem_inc(stored[half], 16)
            sp.sem_inc(m_in[1], 16)
            sp.dma_start(xs[:, 0:TILES, :], x_v[:, 0]).then_inc(x_in, 16)
            for dst, src in ((wq[:], w_qkv), (bq[:], b_qk), (ident[:], ident_in), (tc[:], rope_c), (ts[:], rope_s),
                             (bv[:], b_v.to_broadcast([P, D]))):
                sp.dma_start(dst, src).then_inc(consts_in, 16)
            for b in range(1, B):
                sp.wait_ge(x_in, 16 * b)
                sp.dma_start(xs[:, b * TILES:(b + 1) * TILES, :], x_v[:, b]).then_inc(x_in, 16)
            for dst, src in ((dc[:], dft_c), (dsn[:], dft_s), (dns[:], dft_ns), (wr[:], w_re), (wi[:], w_im),
                             (bf[:], b_ffn.to_broadcast([P, D])), (bo[:], b_out.to_broadcast([P, D])),
                             (wo[:], w_out), (identb[:], identb_in), (mask[:], mask_in)):
                sp.dma_start(dst, src).then_inc(late_in, 16)

            with sp.Fori(0, B) as b:
                for half in range(2):
                    for qk, scr in ((0, q_scr), (1, k_scr)):
                        sp.wait_ge(part2_done, 4 * b + 2 * half + qk + 1)
                        for part in range(PARTS):
                            dst = scr[bass.ds(b, 1), :, half, part].rearrange("o g r t -> (o g) r t")
                            src = parts[:, half, qk, part, :]
                            sp.dma_start(dst, src).then_inc(parts_out[half], 16)
            for half in range(2):
                sp.wait_ge(parts_out[half], 16 * 2 * PARTS * B + 16)

            q_rows = q_scr.rearrange("b g h a (d e) t -> (b g) h (a d) (e t)", d=HD)
            k_rows = k_scr.rearrange("b g h a (d e) t -> (b g) h (a d) (e t)", d=HD)

            def load_q(g, u, half):
                for rep in range(PARTS):
                    dst = qb[rep * PR:(rep + 1) * PR, u, half].rearrange("r e t -> r (e t)")
                    src = q_rows[g, half] if isinstance(g, int) else \
                        q_rows[bass.ds(g, 1), half].rearrange("o r t -> (o r) t")
                    sp.dma_start(dst, src).then_inc(q_in[u][half], 16)

            def load_k(g, u, half):
                rows = k_rows[g, half] if isinstance(g, int) else \
                    k_rows[bass.ds(g, 1), half].rearrange("o r t -> (o r) t")
                for rep in range(PARTS):
                    cut = PR - rep * HD
                    base = rep * PR
                    whole = kb[:, u, half].rearrange("r e t -> r (e t)")
                    sp.dma_start(whole[base:base + cut], rows[rep * HD:PR]).then_inc(k_in[u][half], 16)
                    if rep:
                        sp.dma_start(whole[base + cut:base + PR], rows[0:rep * HD]).then_inc(k_in[u][half], 16)

            sp.wait_ge(zeroed, 2)
            for u in range(2):
                for half in range(2):
                    load_q(u, u, half)
                    load_k(u, u, half)

            def max_rows_to(count, u, half):
                sp.wait_ge(ring_read, count)
                dst = qb[MROW:MROW + PARTS, u, half].rearrange("r e (a q) -> r (e a) q", q=P)
                sp.dma_start(dst, mT[:, half, :]).then_inc(m_in[half], 16)

            max_rows_to(M_END[0] + 1, 0, 0)

            def sp_group(i, u, last):
                g = i * 2 + u
                pos = AT_RING_LAST if last and u == 1 else AT_RING
                base = i * (2 * RING_USES) + RING_USES * u + RING_FIRST + 1
                max_rows_to(base + pos["turned maxima", 1], u, 1)
                if not last:
                    sp.wait_ge(scores_done, i * (2 * NU) + NU * u + UNITS_OF[HT - 1][-1] + 1)
                    load_q(g + 2, u, 0)
                if not (last and u == 1):
                    max_rows_to(base + pos["turned maxima", 0], 1 - u, 0)
                if not last:
                    sp.wait_ge(scores_done, i * (2 * NU) + NU * u + UNITS_OF[2 * HT - 1][-1] + 1)
                    load_k(g + 2, u, 0)
                if not last:
                    sp.wait_ge(scores_done, i * (2 * NU) + NU * (u + 1))
                    load_q(g + 2, u, 1)
                    load_k(g + 2, u, 1)

            with sp.Fori(0, G // 2 - 1) as i:
                for u in range(2):
                    sp_group(i, u, False)
            for u in range(2):
                sp_group(G // 2 - 1, u, True)

            with sp.Fori(0, B) as b:
                for half in range(2):
                    sp.wait_ge(res_done, 2 * b + half + 1)
                    dst = o_v[:, bass.ds(b, 1), half * HT:(half + 1) * HT, :].rearrange("p o t d -> p (o t) d")
                    sp.dma_start(dst, res[half].rearrange("p (t d) -> p t d", d=D)).then_inc(stored[half], 16)
            for half in range(2):
                sp.wait_ge(stored[half], 16 * B + 16)

        @block.gpsimd
        def _(pool):
            pool.memset(qb[:].bitcast(F32), 0.0)
            pool.memset(vres[:], 1.0)
            pool.memset(vpad[:], 0.0)
            pool.memset(mcut[:].bitcast(F32), 0.0).then_inc(zeroed, 1)

            with pool.Fori(0, B) as b:
                for half in range(2):
                    k = 2 * b + half
                    for qk in range(2):
                        pool.wait_ge(proj_read, 5 * k + 2 * qk + 2)
                        pool.tensor_tensor(prod[half][qk][:, 0], prod[half][qk][:, 0], prod[half][qk][:, 1],
                                           ALU.add).then_inc(rot_done, 1)
                    for qk in range(2):
                        pool.wait_ge(part0_done, 2 * k + qk + 1)
                        pool.tensor_tensor(rest[half][qk], prod[half][qk][:, 0], parts[:, half, qk, 0, :],
                                           ALU.subtract).then_inc(rest_done, 1)

            chain = [0]

            def done(ins):
                chain[0] += 1
                ins.then_inc(pool_step, 1)
                return chain[0]

            def cut_max(before, half, max_count):
                at0 = chain[0]

                def own(ins):
                    n = done(ins) - at0
                    pool.wait_ge(pool_step, before + n)
                pool.wait_ge((ring_read, max_joined)[half], max_count)
                m = negm[:, half, :]
                if half == 0:
                    src = mpart[:, 0, 0].rearrange("p e q -> p (e q)")
                else:
                    src = m
                n = HPG * HT
                pool.sem_inc(pool_gate)
                cut = [mcut[:, half, a * n:(a + 1) * n] for a in range(PARTS)]
                own(pool.tensor_copy(cut[0], src))
                own(pool.tensor_tensor(mrest[:, half, :], src, cut[0], ALU.subtract))
                pool.sem_inc(pool_gate)
                own(pool.tensor_copy(cut[1], mrest[:, half, :]))
                pool.tensor_tensor(cut[2], mrest[:, half, :], cut[1], ALU.subtract).then_inc(mcut_done, 1)

            def copy_v(g, u):
                pool.sem_inc(pool_gate)
                src = vres[:, g, :] if isinstance(g, int) else vres[:, bass.ds(g, 1), :].rearrange("p o f -> p (o f)")
                pool.tensor_copy(vpad[:, u, :, :, 0:VC].rearrange("p t e c -> p (t e) c"),
                                 src.rearrange("p (n c) -> p n c", c=VC)).then_inc(v_ready, 1)

            def diagonal(i, u, s):
                for n in UNITS_OF[s]:
                    _, _, heads = UNITS[n]
                    w = STEPS[s][3]
                    pool.wait_ge(exp_done, i * (2 * NU) + NU * u + n + 1)
                    pool.sem_inc(pool_gate)
                    at_slot = pr[:, (NU * u + n) % RING]
                    if heads == 2:
                        view, pat = at_slot[:, :, 0:P], [[0, 2], [1, P]]
                    else:
                        view = at_slot[:, :, 0:2 * w].rearrange("p a (c q) -> p a c q", c=2)[:, :, :, 0:P]
                        pat = [[0, 2], [0, 2], [1, P]]
                    pool.affine_select(out=view, in_=view, compare_op=ALU.is_ge, fill=0.0, base=0,
                                       pattern=pat, channel_multiplier=-1).then_inc(diag_done, 1)

            pool.wait_ge(proj_read, 5 * 2 * B)
            pool.wait_ge(late_in, 16 * LATE)
            copy_v(0, 0)
            cut_max(0, 0, M_END[0])
            for s in range(LEAD):
                diagonal(0, 0, s)

            def add_out_bias(g):
                n = B * TILES // G
                rows = xs[:, bass.ds(g * n, n), :]
                pool.tensor_tensor(rows, rows, bo[:].rearrange("p (o d) -> p o d", o=1).to_broadcast([P, n, D]), ALU.add)

            def pool_group(i, u, last):
                end = last and u == 1
                g = i * 2 + u
                cut_max(i * (2 * 6) + 3 + 6 * u, 1, i * 2 + u + 1)
                for s in range(LEAD, HT):
                    diagonal(i, u, s)
                if not end:
                    cut_max(i * (2 * 6) + 6 + 6 * u, 0, i * (2 * RING_USES) + RING_USES * u + RING_FIRST
                            + AT_RING["max", M_END[0] - 1] + 1)
                    pool.wait_ge(pv_done, i * (2 * NS) + NS * u + NS)
                    copy_v(g + 1, 1 - u)
                add_out_bias(g)
                for s in range(2 * HT, NS):
                    diagonal(i, u, s)
                if not end:
                    nxt = (i, 1) if u == 0 else (i + 1, 0)
                    for s in range(LEAD):
                        diagonal(*nxt, s)

            with pool.Fori(0, G // 2 - 1) as i:
                for u in range(2):
                    pool_group(i, u, False)
            for u in range(2):
                pool_group(G // 2 - 1, u, True)

            with pool.Fori(0, B) as b:
                for half in range(2):
                    pool.wait_ge(ffn_read, 2 * b + half + 3)
                    r3 = res[half].rearrange("p (t d) -> p t d", d=D)
                    pool.tensor_tensor(r3, r3, bf[:].rearrange("p (o d) -> p o d", o=1).to_broadcast([P, HT, D]),
                                       ALU.add).then_inc(res_done, 1)

        @block.tensor
        def _(pe):
            pe.sem_inc(pv_done, NS)
            pe.sem_inc(oraw_done, 2)
            pe.sem_inc(out_proj_read, 2)
            pe.sem_inc(ffn_read, 2)
            pe.wait_ge(consts_in, 16 * EARLY)

            def turn_tokens(b):
                for half in range(2):
                    pe.wait_ge(xn_done, 2 * b + half + 1)
                    for t in range(HT):
                        mm = pe.transpose(ps[:, 6 + half, t * P:(t + 1) * P], xn[:, half, t, :], ident[:])
                    mm.then_inc(xnT_turned, 1)

            def project(b, half):
                k = 2 * b + half
                pe.wait_ge(xnT_done, k + 1)
                if not (isinstance(k, int) and k == 0):
                    pe.wait_ge(proj_read, 5 * k)
                for j in range(4):
                    pe.matmul(ps[:, 1 + j, :], wq[:, j, :], xnT[:, half, :],
                              start=True, stop=True).then_inc(proj_done, 1)
                for t in range(HT):
                    mm = pe.matmul(ps[:, 5, t * P:(t + 1) * P], xnT[:, half, t * P:(t + 1) * P], wq[:, 4, :],
                                   start=(t == 0), stop=True, skip_group_check=True)
                mm.then_inc(proj_done, 1)

            turn_tokens(0)
            project(0, 0)
            with pe.Fori(0, B - 1) as b:
                project(b, 1)
                turn_tokens(b + 1)
                project(b + 1, 0)
            project(B - 1, 1)

            pe.wait_ge(late_in, 16 * LATE)
            pe.wait_ge(proj_read, 5 * 2 * B)
            pe.matmul(ps[:, 0, 0:D], wr[:], dc[:], start=True, stop=False)
            pe.matmul(ps[:, 0, 0:D], wi[:], dsn[:], start=False, stop=True)
            pe.matmul(ps[:, 1, 0:D], wi[:], dc[:], start=True, stop=False)
            pe.matmul(ps[:, 1, 0:D], wr[:], dns[:], start=False, stop=True).then_inc(ffn_a, 1)
            pe.wait_ge(ffn_a_out, 1)
            pe.matmul(ps[:, 2, 0:D], a12[:, 0, :], dc[:], start=True, stop=False)
            pe.matmul(ps[:, 2, 0:D], a12[:, 1, :], dns[:], start=False, stop=True).then_inc(ffn_m, 1)

            def ring_bank(base, pos):
                if not (isinstance(base, int) and base + pos < NRING):
                    pe.wait_ge(ring_read, base + (pos - NRING + 1))
                return RING_BANK[pos % NRING]

            def max_scores(u, m, base, pos):
                half, qt, h0, heads, k0, w, diag, _ = MUNITS[m]
                bank = ring_bank(base, pos)
                for n in range(heads):
                    mm = pe.matmul(ps[:, bank, n * w:(n + 1) * w],
                                   qb[0:MROW, u, half, h0 + n, qt * P:(qt + 1) * P],
                                   kb[0:MROW, u, k0 // HALF, h0 + n, 0:w],
                                   start=(n == 0), stop=not diag, skip_group_check=True)
                if diag:
                    for n in range(heads):
                        mm = pe.matmul(ps[:, bank, (n + 1) * w - P:(n + 1) * w], identb[:], mask[:],
                                       start=False, stop=True, skip_group_check=True)
                mm.then_inc(ring_filled, 1)

            def wait_operands(i, u, half):
                pe.wait_ge(q_in[u][half], i * 48 + 48)
                pe.wait_ge(k_in[u][half], i * 80 + 80)

            def turn_max(base, pos, cuts, half):
                pe.wait_ge(mcut_done, cuts)
                bank = ring_bank(base, pos)
                pe.transpose(ps[:, bank, :].bitcast(BF16)[:, 0:P], mcut[:, half, :], identb[:]).then_inc(ring_filled, 1)

            def scores(i, u, n):
                s, h0, heads = UNITS[n]
                half, kt, c0, w, _ = STEPS[s]
                if not (isinstance(i, int) and i == 0 and u == 0 and n < 2):
                    pe.wait_ge(exp_done, i * (2 * NU) + NU * u + n - 1)
                bank = S_BANK[n % 2]
                per = heads // 2
                for m in range(heads):
                    col = (m % per) * w
                    mm = pe.matmul(ps[:, bank + m // per, col:col + w],
                                   kb[0:SROWS, u, kt // HT, h0 + m, (kt % HT) * P:(kt % HT + 1) * P],
                                   qb[0:SROWS, u, half, h0 + m, c0:HALF],
                                   start=(m % per == 0), stop=True, skip_group_check=True)
                mm.then_inc(scores_done, 1)

            def value_step(i, u, s):
                half, kt, c0, w, diag = STEPS[s]
                n = UNITS_OF[s][-1]
                if diag:
                    pe.wait_ge(diag_done, i * (2 * ND) + ND * u + DIAG.index(n) + 1)
                else:
                    pe.wait_ge(exp_done, i * (2 * NU) + NU * u + n + 1)
                if kt == 0:
                    pe.wait_ge(oraw_done, i * 4 + 2 * u + half + 2)
                if s == 0:
                    pe.wait_ge(v_ready, i * 2 + u + 1)
                for e in range(HPG):
                    if len(UNITS_OF[s]) == 2:
                        slot, src = (NU * u + UNITS_OF[s][e // 2]) % RING, (e % 2, 0)
                    else:
                        slot, src = (NU * u + n) % RING, (e // 2, (e % 2) * w)
                    mm = pe.matmul(ps[32 * e:32 * e + 32, PV_BANK, c0:HALF], vpad[:, u, kt, e, :],
                                   pr[:, slot, src[0], src[1]:src[1] + w],
                                   start=(kt == 0), stop=(s in HALF_END), skip_group_check=True)
                mm.then_inc(pv_done, 1)

            def turn_out(i, u, half, base, pos):
                pe.wait_ge(oraw_done, i * 4 + 2 * u + half + 3)
                bank = ring_bank(base, pos)
                for t in range(HT):
                    mm = pe.transpose(ps[:, bank, t * P:(t + 1) * P], oraw[:, half, t * P:(t + 1) * P], ident[:])
                mm.then_inc(ring_filled, 1)

            pe.wait_ge(zeroed, 2)
            for half in range(2):
                wait_operands(0, 0, half)
                for m in range(M_END[half - 1] if half else 0, M_END[half]):
                    max_scores(0, m, 0, FIRST_POS[m])
                if half == 0:
                    turn_max(0, M_END[0], 1, 0)
            pe.wait_ge(ffn_m_out, 1)
            pe.wait_ge(m_in[0], 16)
            for s in range(LEAD):
                for n in UNITS_OF[s]:
                    scores(0, 0, n)

            def pe_group(i, u, last):
                end = last and u == 1
                nxt = (i, 1) if u == 0 else (i + 1, 0)
                pos = AT_RING_LAST if end else AT_RING
                base = i * (2 * RING_USES) + RING_USES * u + RING_FIRST
                for s in range(NS):
                    a = s + LEAD
                    if a < NS:
                        if a == HT:
                            pe.wait_ge(m_in[1], i * 32 + 16 * u + 32)
                        units = [(i, u, n) for n in UNITS_OF[a]]
                    elif not end:
                        if a == NS:
                            pe.wait_ge(m_in[0], i * 32 + 16 * u + 32)
                        units = [(*nxt, n) for n in UNITS_OF[a - NS]]
                    else:
                        units = []
                    maxima = [] if end else list(range(M_AT[s], M_AT[s + 1]))

                    def some_maxima(count):
                        for m in maxima[:count]:
                            if m == 0:
                                wait_operands(*nxt, 0)
                            if m == M_END[0]:
                                wait_operands(*nxt, 1)
                            max_scores(1 - u, m, base, pos["max", m])
                        del maxima[:count]

                    if s in HALF_END:
                        value_step(i, u, s)
                    for n in units:
                        some_maxima(1)
                        scores(*n)
                    if s not in HALF_END:
                        some_maxima(1)
                        value_step(i, u, s)
                    some_maxima(NM)
                    if s == 0:
                        turn_max(base, pos["turned maxima", 1], i * 4 + 2 * u + 2, 1)
                    if s == A_T0:
                        turn_out(i, u, 0, base, pos["turned outputs", 0])
                    if s == M_T0 and not end:
                        turn_max(base, pos["turned maxima", 0], i * 4 + 2 * u + 3, 0)
                    if s == NS - 1:
                        turn_out(i, u, 1, base, pos["turned outputs", 1])

            with pe.Fori(0, G // 2 - 1) as i:
                for u in range(2):
                    pe_group(i, u, False)
            for u in range(2):
                pe_group(G // 2 - 1, u, True)

            pe.wait_ge(exp_done, NU * G)
            with pe.Fori(0, B) as b:
                for half in range(2):
                    pe.wait_ge(at_done, 2 * b + half + 1)
                    for t in range(HT):
                        mm = pe.transpose(ps[:, half, t * P:(t + 1) * P], at[half][:, t * P:(t + 1) * P], ident[:])
                    mm.then_inc(a_turned, 1)
                for half in range(2):
                    pe.wait_ge(aT_done, 2 * b + half + 1)
                    pe.wait_ge(out_proj_read, 2 * b + half + 1)
                    for t in range(HT):
                        mm = pe.matmul(ps[:, 2 + half, t * P:(t + 1) * P], aT[half][:, t * P:(t + 1) * P], wo[:],
                                       start=(t == 0), stop=True, skip_group_check=True)
                    mm.then_inc(out_proj_done, 1)
            with pe.Fori(0, B) as b:
                for half in range(2):
                    pe.wait_ge(yn_done, 2 * b + half + 1)
                    for t in range(HT):
                        mm = pe.transpose(ps[:, half, t * P:(t + 1) * P], yn[half][:, t * P:(t + 1) * P], ident[:])
                    mm.then_inc(y_turned, 1)
                for half in range(2):
                    pe.wait_ge(ynT_done, 2 * b + half + 1)
                    pe.wait_ge(ffn_read, 2 * b + half + 1)
                    for t in range(HT):
                        mm = pe.matmul(ps[:, 4 + half, t * P:(t + 1) * P], ynT[half][:, t * P:(t + 1) * P], mffn[:],
                                       start=(t == 0), stop=True, skip_group_check=True)
                    mm.then_inc(ffn_done, 1)

        @block.scalar
        def _(act):
            def root(b):
                act.wait_ge(var_done, b + 1)
                act.activation(rstd[:], rstd[:], ACT.Sqrt).then_inc(std_done, 1)

            def tokens_out(b):
                for half in range(2):
                    act.wait_ge(xnT_turned, 2 * b + half + 1)
                    act.copy(xnT[:, half, :], ps[:, 6 + half, :]).then_inc(xnT_done, 1)

            def cut_parts(b, last):
                for half in range(2):
                    act.wait_ge(parts_out[half], b * (16 * 2 * PARTS) + 16)
                    for qk in range(2):
                        act.wait_ge(rot_done, 4 * b + 2 * half + qk + 1)
                        act.copy(parts[:, half, qk, 0, :], prod[half][qk][:, 0]).then_inc(part0_done, 1)
                    if half == 0 and not last:
                        root(b + 1)
                for half in range(2):
                    for qk in range(2):
                        act.wait_ge(rest_done, 4 * b + 2 * half + qk + 1)
                        act.copy(parts[:, half, qk, 1, :], rest[half][qk]).then_inc(part1_done, 1)
                    if half == 0 and not last:
                        tokens_out(b + 1)

            root(0)
            tokens_out(0)
            with act.Fori(0, B - 1) as b:
                cut_parts(b, False)
            cut_parts(B - 1, True)

            act.wait_ge(ffn_a, 1)
            act.activation(a12[:], ps[:, 0:2, 0:D], ACT.Copy, scale=1.0 / D).then_inc(ffn_a_out, 1)
            act.wait_ge(ffn_m, 1)
            act.copy(mffn[:], ps[:, 2, 0:D]).then_inc(ffn_m_out, 1)

            def exp(i, u, n):
                s, _, heads = UNITS[n]
                w = STEPS[s][3]
                act.wait_ge(scores_done, i * (2 * NU) + NU * u + n + 1)
                behind = NU * u + n - RING
                if isinstance(i, int) and 2 * NU * i + behind < 0:
                    pass
                else:
                    step = NS * (behind // NU) + UNITS[behind % NU][0] + 1
                    act.wait_ge(pv_done, i * (2 * NS) + NS + step)
                wide = w * heads // 2
                act.activation(pr[:, (NU * u + n) % RING, :, 0:wide], ps[:, S_BANK[n % 2]:S_BANK[n % 2] + 2, 0:wide],
                               ACT.Exp, scale=SCALE).then_inc(exp_done, 1)

            for s in range(LEAD):
                for n in UNITS_OF[s]:
                    exp(0, 0, n)

            def act_group(i, u, last):
                end = last and u == 1
                nxt = (i, 1) if u == 0 else (i + 1, 0)
                for s in range(NS):
                    if s in HALF_END:
                        half = HALF_END.index(s)
                        act.wait_ge(pv_done, i * (2 * NS) + NS + NS * u + s + 1)
                        act.copy(oraw[:, half, :], ps[:, PV_BANK, :]).then_inc(oraw_done, 1)
                    a = s + LEAD
                    if a < NS:
                        for n in UNITS_OF[a]:
                            exp(i, u, n)
                    elif not end:
                        for n in UNITS_OF[a - NS]:
                            exp(*nxt, n)

            with act.Fori(0, G // 2 - 1) as i:
                for u in range(2):
                    act_group(i, u, False)
            for u in range(2):
                act_group(G // 2 - 1, u, True)

            act.wait_ge(ring_read, RING_FIRST + RING_USES * (G - 1) + len(AT_RING_LAST))
            def outputs_in(b):
                for half in range(2):
                    if not (isinstance(b, int) and b == 0):
                        act.wait_ge(a_turned, 2 * b + half - 1)
                        act.sem_inc(act_gate)
                    src = attn[:, bass.ds(b * HG, HG), half * HT:(half + 1) * HT, :] if not isinstance(b, int) else \
                        attn[:, b * HG:(b + 1) * HG, half * HT:(half + 1) * HT, :]
                    act.copy(at[half].rearrange("p (t g c) -> p g t c", g=HG, t=HT), src).then_inc(at_done, 1)

            def turned_out(b):
                for half in range(2):
                    act.wait_ge(a_turned, 2 * b + half + 1)
                    act.copy(aT[half], ps[:, half, :]).then_inc(aT_done, 1)

            outputs_in(0)
            with act.Fori(0, B - 1) as b:
                turned_out(b)
                outputs_in(b + 1)
            turned_out(B - 1)
            act.wait_ge(var3_done, B)
            act.activation(rs3[:], rs3[:], ACT.Sqrt).then_inc(std3_done, 1)
            with act.Fori(0, B) as b:
                for half in range(2):
                    act.wait_ge(y_turned, 2 * b + half + 1)
                    act.copy(ynT[half], ps[:, half, :]).then_inc(ynT_done, 1)

        @block.vector
        def _(dve):
            def own(ins, count):
                ins.then_inc(dve_step, 1)
                dve.wait_ge(dve_step, count)

            dve.memset(kb[:, :, :, :, :].rearrange("p u h e t -> p (u h e t)").bitcast(F32), 0.0)
            own(dve.memset(mpart[:], 0.0), 1)
            dve.memset(kb[MROW:P].rearrange("p u h e t -> p (u h e t)"), 1.0).then_inc(zeroed, 1)

            def stats(b):
                dve.wait_ge(x_in, 16 * b + 16)
                dve.sem_inc(dve_gate)
                for t in range(TILES):
                    ins = dve.bn_stats(st[:, t, :], xs[:, bass.ds(b * TILES + t, 1), :].rearrange("p o d -> p (o d)"))
                own(ins, 3 * b + 2)
                dve.sem_inc(dve_gate)
                for t in range(TILES):
                    ins = dve.bn_aggr(mv[:, t, :], st[:, t, :])
                own(ins, 3 * b + 3)
                dve.tensor_scalar(rstd[:], mv[:, :, 1], EPS, None, ALU.add).then_inc(var_done, 1)

            def norm(b):
                dve.wait_ge(std_done, b + 1)
                own(dve.reciprocal(rstd[:], rstd[:]), 3 * b + 4)
                for half in range(2):
                    for t in range(HT):
                        j = half * HT + t
                        ins = dve.tensor_scalar(xn[:, half, t, :],
                                                xs[:, bass.ds(b * TILES + j, 1), :].rearrange("p o d -> p (o d)"),
                                                mv[:, j, 0:1], rstd[:, j:j + 1], ALU.subtract, ALU.mult)
                    ins.then_inc(xn_done, 1)

            def rotate(b, half):
                k = 2 * b + half
                for j in range(4):
                    dve.wait_ge(proj_done, 5 * k + j + 1)
                    dve.scalar_tensor_tensor(out=prod[half][j // 2][:, j % 2], in0=ps[:, 1 + j, :],
                                             scalar=bq[:, j:j + 1],
                                             in1=(tc, ts)[j % 2][:, half * HALF:(half + 1) * HALF],
                                             op0=ALU.add, op1=ALU.mult).then_inc(proj_read, 1)
                dve.wait_ge(proj_done, 5 * k + 5)
                for t in range(HT):
                    dst = vres[:, bass.ds(b * HG, HG), :].rearrange("p g (t e c) -> p g t e c", e=HPG, c=VC)[
                        :, :, half * HT + t, :, 0:HD]
                    ins = dve.tensor_tensor(dst, ps[:, 5, t * P:(t + 1) * P].rearrange("p (g e c) -> p g e c", e=HPG, c=HD),
                                            bv[:].rearrange("p (g e c) -> p g e c", e=HPG, c=HD), ALU.add)
                ins.then_inc(proj_read, 1)

            def batch(b, last):
                rotate(b, 0)
                if not last:
                    stats(b + 1)
                rotate(b, 1)
                if not last:
                    norm(b + 1)
                for half in range(2):
                    for qk in range(2):
                        dve.wait_ge(part1_done, 4 * b + 2 * half + qk + 1)
                        dve.tensor_tensor(parts[:, half, qk, 2, :], rest[half][qk], parts[:, half, qk, 1, :],
                                          ALU.subtract).then_inc(part2_done, 1)

            stats(0)
            norm(0)
            dve.wait_ge(consts_in, 16 * EARLY)
            dve.wait_ge(zeroed, 2)
            with dve.Fori(0, B - 1) as b:
                batch(b, False)
            batch(B - 1, True)
            n1 = 1 + 3 * B

            def take_max(m, base, pos):
                half, qt, h0, heads, _, w, _, which = MUNITS[m]
                dve.wait_ge(ring_filled, base + (pos + 1))
                dve.tensor_reduce(mpart[:, half, which, h0:h0 + heads, qt],
                                  ps[:, RING_BANK[pos % NRING], 0:heads * w].rearrange("p (e k) -> p e k", e=heads),
                                  AX_X, ALU.max, negate=True).then_inc(ring_read, 1)
                if m == NM - 1:
                    dve.wait_ge(ring_read, base + (pos + 1))
                    dve.tensor_tensor(negm[:, 1, :], mpart[:, 1, 0].rearrange("p e q -> p (e q)"),
                                      mpart[:, 1, 1].rearrange("p e q -> p (e q)"), ALU.min).then_inc(max_joined, 1)

            def max_row_out(base, pos, half, rows):
                dve.wait_ge(ring_filled, base + (pos + 1))
                if rows is not None:
                    dve.wait_ge(m_in[half], rows)
                n = PARTS * HPG * HT
                dve.tensor_copy(mT[:, half, :],
                                ps[0:n, RING_BANK[pos % NRING], :].bitcast(BF16)[:, 0:P]).then_inc(ring_read, 1)

            def outputs(i, u, half, base, pos, own_count):
                dve.wait_ge(ring_filled, base + (pos + 1))
                o = ps[:, RING_BANK[pos % NRING], :].rearrange("p (t e c) -> p t e c", t=HT, c=32)
                own(dve.reciprocal(rden[:, half], o[:, :, :, HD]), own_count)
                g = i * 2 + u
                dst = attn[:, bass.ds(g, 1), half * HT:(half + 1) * HT, :] if not isinstance(g, int) else \
                    attn[:, g:g + 1, half * HT:(half + 1) * HT, :]
                dst = dst.rearrange("p o t (e c) -> p (o t) e c", c=HD)
                dve.tensor_tensor(dst, o[:, :, :, 0:HD],
                                  rden[:, half].rearrange("p t (e o) -> p t e o", o=1).to_broadcast([P, HT, HPG, HD]),
                                  ALU.mult).then_inc(ring_read, 1)

            for m in range(NM):
                if m == M_END[0]:
                    max_row_out(0, M_END[0], 0, None)
                take_max(m, 0, FIRST_POS[m])

            def dve_group(i, u, last):
                end = last and u == 1
                pos = AT_RING_LAST if end else AT_RING
                base = i * (2 * RING_USES) + RING_USES * u + RING_FIRST
                for s in range(NS):
                    if not end:
                        for m in range(M_AT[s], M_AT[s + 1]):
                            take_max(m, base, pos["max", m])
                    if s == 0:
                        max_row_out(base, pos["turned maxima", 1], 1, i * 32 + 16 * u + 16)
                    if s == A_T0:
                        outputs(i, u, 0, base, pos["turned outputs", 0], i * 4 + n1 + 2 * u + 1)
                    if s == M_T0 and not end:
                        max_row_out(base, pos["turned maxima", 0], 0, i * 32 + 16 * u + 16)
                    if s == NS - 1:
                        outputs(i, u, 1, base, pos["turned outputs", 1], i * 4 + n1 + 2 * u + 2)

            with dve.Fori(0, G // 2 - 1) as i:
                for u in range(2):
                    dve_group(i, u, False)
            for u in range(2):
                dve_group(G // 2 - 1, u, True)
            n2 = n1 + 2 * G

            with dve.Fori(0, B) as b:
                for half in range(2):
                    dve.wait_ge(out_proj_done, 2 * b + half + 1)
                    rows = xs[:, bass.ds(b * TILES + half * HT, HT), :]
                    dve.tensor_tensor(rows, rows, ps[:, 2 + half, :].rearrange("p (t d) -> p t d", d=D),
                                      ALU.add).then_inc(out_proj_read, 1)
                    dve.wait_ge(out_proj_read, 2 * b + half + 3)
                    dve.sem_inc(dve_gate)
                    for t in range(HT):
                        j = half * HT + t
                        ins = dve.bn_stats(st3[:, j, :],
                                           xs[:, bass.ds(b * TILES + j, 1), :].rearrange("p o d -> p (o d)"))
                own(ins, 2 * b + (n2 + 1))
                dve.sem_inc(dve_gate)
                for t in range(TILES):
                    ins = dve.bn_aggr(mv3[:, t, :], st3[:, t, :])
                own(ins, 2 * b + (n2 + 2))
                dve.tensor_scalar(rs3[:, bass.ds(b * TILES, TILES)], mv3[:, :, 1], EPS, None, ALU.add)
                dve.tensor_copy(mean3[:, bass.ds(b * TILES, TILES)], mv3[:, :, 0]).then_inc(var3_done, 1)

            dve.wait_ge(std3_done, 1)
            own(dve.reciprocal(rs3[:], rs3[:]), n2 + 2 * B + 1)

            def norm3(b):
                for half in range(2):
                    if not (isinstance(b, int) and b == 0):
                        dve.wait_ge(y_turned, 2 * b + half - 1)
                    for t in range(HT):
                        j = b * TILES + half * HT + t
                        ins = dve.tensor_scalar(yn[half][:, t * P:(t + 1) * P],
                                                xs[:, bass.ds(j, 1), :].rearrange("p o d -> p (o d)"),
                                                mean3[:, bass.ds(j, 1)], rs3[:, bass.ds(j, 1)],
                                                ALU.subtract, ALU.mult)
                    ins.then_inc(yn_done, 1)

            def finish(b):
                for half in range(2):
                    dve.wait_ge(stored[half], 16 * b + 16)
                    dve.wait_ge(ffn_done, 2 * b + half + 1)
                    dve.tensor_tensor(res[half].rearrange("p (t d) -> p t d", d=D),
                                      xs[:, bass.ds(b * TILES + half * HT, HT), :],
                                      ps[:, 4 + half, :].rearrange("p (t d) -> p t d", d=D),
                                      ALU.add).then_inc(ffn_read, 1)

            norm3(0)
            with dve.Fori(0, B - 1) as b:
                norm3(b + 1)
                finish(b)
            finish(B - 1)


def kernel(**inputs):
    import numpy as np
    import concourse.bacc as bacc
    from concourse.bass_utils import run_bass_kernel_spmd as run

    x = np.ascontiguousarray(inputs["L0_attn_x"])
    w = np.asarray(inputs["L0_attn_qkv_w"])
    bias = np.asarray(inputs["L0_attn_qkv_b"])

    g, d, e = np.meshgrid(np.arange(HG), np.arange(HD), np.arange(HPG), indexing="ij")
    even = 2 * (d % (HD // 2)) + d // (HD // 2)
    odd = 2 * (d % (HD // 2)) + 1 - d // (HD // 2)
    head = (g * HPG + e) * HD
    straight, swapped = (head + even).reshape(-1), (head + odd).reshape(-1)
    cols = [straight, swapped, D + straight, D + swapped]
    w_qkv = np.ascontiguousarray(np.stack([w[:, c] for c in cols] + [w[:, 2 * D:]], axis=1))
    b_qk = np.ascontiguousarray(np.stack([bias[c] for c in cols], axis=1))

    f = (np.float32(1.0) / np.float32(10000.0) ** (np.arange(0, HD, 2, dtype=np.float32) / np.float32(HD))).astype(np.float32)
    angle = (np.arange(T, dtype=np.float32)[:, None] * f[None, :]).astype(np.float64)
    rope = np.concatenate([np.sin(angle), np.cos(angle)], axis=-1)
    sin, cos = rope[:, 0::2], rope[:, 1::2]
    dim = d.reshape(-1)
    rope_c = np.ascontiguousarray(cos[:, dim % 4].T.astype(np.float32))
    rope_s = np.ascontiguousarray((sin[:, dim % 4] * np.where(dim < 4, -1.0, 1.0)).T.astype(np.float32))
    k = np.arange(D)
    turn = 2 * np.pi * (k[:, None] * k[None, :] % D) / D
    dft_c, dft_s = np.cos(turn).astype(np.float32), np.sin(turn).astype(np.float32)
    eye = np.eye(P, dtype=np.float32)
    bf = mybir.dt.np(BF16)
    future = np.where(np.arange(P)[None, :] > np.arange(P)[:, None], NEG, 0.0).astype(bf)

    nc = bacc.Bacc("TRN2", target_bir_lowering=False, num_devices=1)
    arrays, args = {}, []
    for name, a in (("x", x), ("w_qkv", w_qkv), ("b_qk", b_qk), ("b_v", bias[None, 2 * D:]),
                    ("w_out", inputs["L0_attn_out_w"]), ("b_out", np.asarray(inputs["L0_attn_out_b"])[None, :]),
                    ("w_re", inputs["L0_ffn_w_freq_real"]), ("w_im", inputs["L0_ffn_w_freq_imag"]),
                    ("b_ffn", np.asarray(inputs["L0_ffn_bias"])[None, :]),
                    ("rope_c", rope_c), ("rope_s", rope_s), ("dft_c", dft_c), ("dft_s", dft_s), ("dft_ns", -dft_s),
                    ("ident", eye), ("identb", eye.astype(bf)), ("mask", future)):
        a = np.ascontiguousarray(a)
        arrays[f"in_{name}"] = a
        args.append(nc.dram_tensor(f"in_{name}", a.shape, mybir.dt.from_np(a.dtype), kind="ExternalInput").ap())
    for name in ("q_scr", "k_scr"):
        args.append(nc.dram_tensor(name, (B, HG, 2, PARTS, HD * HPG, HALF), BF16, kind="Internal").ap())
    args.append(nc.dram_tensor("out_0", (B, T, D), F32, kind="ExternalOutput").ap())
    build(nc, *args)
    r = run(nc, [arrays], core_ids=[0])
    return r.results[0]["out_0"]
```

```python
from contextlib import ExitStack

import concourse.bass as bass
from concourse import mybir

F32 = mybir.dt.float32
BF16 = mybir.dt.bfloat16
ACT = mybir.ActivationFunctionType
ALU = mybir.AluOpType
AX_X = mybir.AxisListType.X

P = 128
B, T, D = 4, 1024, 128
H, HD = 16, 8
HPG = 4
HG = H // HPG
G = B * HG
TILES = T // P
HALF = 512
HT = HALF // P
PARTS = 3
PR = PARTS * HD
KROWS = PARTS * PR
MROW = 96
SROWS = MROW + PARTS
VC = HD + 1
EPS = 1e-5
SCALE = float(HD) ** -0.5
NEG = -1e38

STEPS = []
for half in range(2):
    for kt in range(HT * (half + 1)):
        c0 = max(0, kt - HT * half) * P
        STEPS.append((half, kt, c0, HALF - c0, kt >= HT * half))
NS = len(STEPS)
UNITS = []
for s, (_, _, _, w, _) in enumerate(STEPS):
    UNITS += [(s, 0, 4)] if 2 * w <= HALF else [(s, 0, 2), (s, 2, 2)]
NU = len(UNITS)
UNITS_OF = [[n for n, u in enumerate(UNITS) if u[0] == s] for s in range(NS)]
DIAG = [n for n, u in enumerate(UNITS) if STEPS[u[0]][4]]
ND = len(DIAG)
LEAD = 2
RING = 8
HALF_END = [HT - 1, NS - 1]
assert NU % 2 == 0 and 2 * NU % RING == 0

MUNITS = []
for qt in range(HT):
    w = (qt + 1) * P
    n = HALF // w
    n = 4 if n >= 4 else 2 if n >= 2 else 1
    MUNITS += [(0, qt, h, n, 0, w, True, 0) for h in range(0, HPG, n)]
for qt in range(HT):
    w = (qt + 1) * P
    n = HALF // w
    n = 4 if n >= 4 else 2 if n >= 2 else 1
    MUNITS += [(1, qt, h, 1, 0, HALF, False, 0) for h in range(HPG)]
    MUNITS += [(1, qt, h, n, HALF, w, True, 1) for h in range(0, HPG, n)]
NM = len(MUNITS)
M_END = [sum(1 for m in MUNITS if m[0] == 0), NM]
assert NM % 2 == 0
M_PLAN = [
    [1, 2, 0],
    [1, 3, 1],
    [2, 1, 1, 0],
    [0, 1, 1, 1],
    [2, 1, 1, 1],
    [0, 1, 1, 1],
    [0, 1, 0, 1],
    [0, 1, 1, 1],
    [0, 1, 2],
    [1, 0, 0],
    [1, 2, 1, 0],
    [0, 1, 1, 0],
]
M_AT = [sum(sum(p) for p in M_PLAN[:s]) for s in range(NS + 1)]
A_T0 = 6
M_T0 = 7
assert M_AT[M_T0 + 1] >= M_END[0] and M_AT[NS] == NM
def _ring_order(last):
    order = []
    for s in range(NS):
        if not last:
            order += [("max", m) for m in range(M_AT[s], M_AT[s + 1])]
        if last:
            order += [("turned attention", s)] * (s < EARLY_HALVES)
            order += [("projection", s - 1)] * (0 <= s - 1 < EARLY_HALVES)
        order += [("turned maxima", 1)] * (s == 0) + [("turned outputs", 0)] * (s == A_T0)
        if not last:
            order += [("turned maxima", 0)] * (s == M_T0)
        order += [("turned outputs", 1)] * (s == NS - 1)
    return {use: n for n, use in enumerate(order)}


EARLY_HALVES = 2 * (B - 1)
assert EARLY_HALVES < NS - 1
NRING = 3
AT_RING = _ring_order(False)
AT_RING_LAST = _ring_order(True)
RING_USES = len(AT_RING)
RING_FIRST = NM + 1
assert RING_USES % NRING == 0 and RING_FIRST % NRING == 0
FIRST_TURN = M_END[0] + 2 * NRING
FIRST_POS = {m: m if m < FIRST_TURN else m + 1 for m in range(NM)}
FFN_AT = FIRST_TURN + 4


def build(nc, x, w_qkv, b_qk, b_v, w_out, b_out, w_re, w_im, b_ffn,
          rope_c, rope_s, dft_c, dft_s, dft_ns, ident_in, identb_in, mask_in, pad_in, q_scr, k_scr, out):
    with ExitStack() as ctx:
        def sb(name, shape, dt=F32):
            return ctx.enter_context(nc.sbuf_tensor(name, shape, dt))

        def sem(name):
            return ctx.enter_context(nc.semaphore(name))

        wq = sb("wq", [P, 5, P])
        bq = sb("bq", [P, 4])
        bv = sb("bv", [P, 1])
        bvw = sb("bvw", [P, D])
        wo = sb("wo", [P, D])
        bo = sb("bo", [P, D])
        bf = sb("bf", [P, D])
        wr = sb("wr", [P, D])
        wi = sb("wi", [P, D])
        tc = sb("tc", [P, T])
        ts = sb("ts", [P, T])
        dc = sb("dc", [P, D])
        dsn = sb("dsn", [P, D])
        dns = sb("dns", [P, D])
        ident = sb("ident", [P, P])
        identb = sb("identb", [P, P], BF16)
        mask = sb("mask", [P, P], BF16)
        a12 = sb("a12", [P, 2, D])
        mffn = sb("mffn", [P, D])
        xs = sb("xs", [P, B * TILES, D])
        attn = sb("attn", [P, G, TILES, HPG * HD])
        vres = sb("vres", [P, G, TILES * HPG * VC])
        st = sb("st", [P, TILES, 6])
        mv = sb("mv", [P, TILES, 2])
        rstd = sb("rstd", [P, TILES])
        xn = sb("xn", [P, 2, HT, D])
        xnT = sb("xnT", [P, 2, HALF])
        parts = sb("parts", [P, 2, 2, PARTS, HALF], BF16)
        qb = sb("qb", [P, 2, 2, HPG, HALF], BF16)
        kb = sb("kb", [P, 2, 2, HPG, HALF], BF16)
        vpad = sb("vpad", [P, 2, TILES, HPG, 32])
        pr = sb("pr", [P, RING, 2, HALF])
        oraw = sb("oraw", [P, 2, HALF])
        mpart = sb("mpart", [P, 2, 2, HPG, HT])
        negm = sb("negm", [P, 2, HPG * HT])
        mrest = sb("mrest", [P, 2, HPG * HT])
        mcut = sb("mcut", [P, 2, P], BF16)
        mT = sb("mT", [PARTS * HPG * HT, 2, P], BF16)
        rden = sb("rden", [P, 2, HT, HPG])
        at_early = sb("at_early", [P, EARLY_HALVES, HALF])
        aT_early = sb("aT_early", [P, 2, HALF])
        st3 = sb("st3", [P, TILES, 6])
        mv3 = sb("mv3", [P, TILES, 2])
        mean3 = sb("mean3", [P, B * TILES])
        table_probe = sb("table_probe", [P, 1])
        rs3 = sb("rs3", [P, B * TILES])

        prod = [[pr[:, 2 * half + qk] for qk in range(2)] for half in range(2)]
        rest = [[pr[:, 4 + half, qk, :] for qk in range(2)] for half in range(2)]
        at, aT = ([pr[:, 2 * n + half, 0, :] for half in range(2)] for n in range(2))
        yn, ynT = ([at_early[:, 2 * n + half, :] for half in range(2)] for n in range(2))

        ps = ctx.enter_context(nc.psum_tensor("ps", [P, 8, HALF], F32))

        S_BANK = [0, 2]
        PV_BANK = 6
        RING_BANK = [4, 7, 5]
        V_BANK = [5, 0]

        x_in = sem("x_in")
        consts_in = sem("consts_in")
        zeroed = sem("zeroed")
        ffn_a = sem("ffn_a")
        ffn_a_out = sem("ffn_a_out")
        ffn_m = sem("ffn_m")
        ffn_m_out = sem("ffn_m_out")
        dve_step = sem("dve_step")
        pool_step = sem("pool_step")
        var_done = sem("var_done")
        std_done = sem("std_done")
        xn_done = sem("xn_done")
        xnT_turned = sem("xnT_turned")
        xnT_done = sem("xnT_done")
        proj_done = sem("proj_done")
        proj_read = sem("proj_read")
        rot_done = sem("rot_done")
        part0_done = sem("part0_done")
        rest_done = sem("rest_done")
        part2_done = sem("part2_done")
        parts_out = [sem("parts_out0"), sem("parts_out1")]
        q_in = [[sem(f"q_in{u}{h}") for h in range(2)] for u in range(2)]
        k_in = [[sem(f"k_in{u}{h}") for h in range(2)] for u in range(2)]
        m_in = [sem("m_in0"), sem("m_in1")]
        ring_filled = sem("ring_filled")
        ring_read = sem("ring_read")
        max_joined = sem("max_joined")
        mcut_done = sem("mcut_done")
        scores_done = sem("scores_done")
        exp_done = sem("exp_done")
        diag_done = sem("diag_done")
        v_ready = sem("v_ready")
        pv_done = sem("pv_done")
        oraw_done = sem("oraw_done")
        at_early_done = sem("at_early_done")
        stats_step = sem("stats_step")
        at_done = sem("at_done")
        a_turned = sem("a_turned")
        aT_done = sem("aT_done")
        out_proj_done = sem("out_proj_done")
        out_proj_read = sem("out_proj_read")
        var3_done = sem("var3_done")
        std3_done = sem("std3_done")
        yn_done = sem("yn_done")
        y_turned = sem("y_turned")
        ynT_done = sem("ynT_done")
        ffn_done = sem("ffn_done")
        ffn_read = sem("ffn_read")
        ffn_bias_done = sem("ffn_bias_done")
        stored = [sem("stored0"), sem("stored1")]
        part1_done = sem("part1_done")
        v_read = sem("v_read")
        bias_done = sem("bias_done")
        bias_row = sem("bias_row")
        bias_ready = sem("bias_ready")
        late_in = sem("late_in")
        act_gate = sem("act_gate")
        pool_gate = sem("pool_gate")
        dve_gate = sem("dve_gate")

        EARLY, LATE = 6, 12
        x_v = x.rearrange("b (t p) d -> p b t d", p=P)
        o_v = out.rearrange("b (t p) d -> p b t d", p=P)

        block = ctx.enter_context(nc.Block())

        @block.sync
        def _(sp):
            for half in range(2):
                sp.sem_inc(parts_out[half], 16)
            sp.sem_inc(m_in[1], 16)
            sp.dma_start(xs[:, 0:TILES, :], x_v[:, 0]).then_inc(x_in, 16)
            for dst, src in ((wq[:], w_qkv), (bq[:], b_qk), (ident[:], ident_in), (tc[:], rope_c), (ts[:], rope_s),
                             (bv[:], b_v)):
                sp.dma_start(dst, src).then_inc(consts_in, 16)
            for b in range(1, B):
                sp.wait_ge(x_in, 16 * b)
                sp.dma_start(xs[:, b * TILES:(b + 1) * TILES, :], x_v[:, b]).then_inc(x_in, 16)
            for dst, src in ((dc[:], dft_c), (dsn[:], dft_s), (dns[:], dft_ns), (wr[:], w_re), (wi[:], w_im),
                             (bf[:], b_ffn.to_broadcast([P, D])), (bo[:], b_out.to_broadcast([P, D])),
                             (wo[:], w_out), (identb[:], identb_in), (mask[:], mask_in),
                             (kb[KROWS:SROWS].rearrange("p u h e t -> p (u h e t)"), pad_in),
                             (qb[KROWS:MROW].rearrange("p u h e t -> p (u h e t)"), pad_in[0:MROW - KROWS])):
                sp.dma_start(dst, src).then_inc(late_in, 16)

            q_rows = q_scr.rearrange("h a b g (d e) t -> h (b g) a d (e t)", d=HD)
            k_rows = k_scr.rearrange("h a b g (d e) t -> h (b g) a d (e t)", d=HD)

            def load_q(g, u, half):
                for part in range(PARTS):
                    src = q_rows[half, bass.ds(g, 1), part]
                    dst = qb[part * PR:(part + 1) * PR, u, half].rearrange("r e t -> r (e t)")
                    sp.dma_start(dst, src.to_broadcast([PARTS, HD, HPG * HALF])).then_inc(q_in[u][half], 16)

            def load_k(g, u, half):
                for rep in range(PARTS):
                    src = k_rows[half, bass.ds(g, 1)].rearrange("o a d f -> (o a) d f")
                    dst = kb[rep * PR:(rep + 1) * PR, u, half].rearrange("r e t -> r (e t)")
                    sp.dma_start(dst, src).then_inc(k_in[u][half], 16)

            def store_parts(b):
                for half in range(2):
                    for qk, scr in ((0, q_scr), (1, k_scr)):
                        sp.wait_ge(part2_done, 4 * b + 2 * half + qk + 1)
                        dst = scr[half, :, bass.ds(b, 1)].rearrange("a o g r t -> (o g r) a t")
                        sp.dma_start(dst, parts[:, half, qk]).then_inc(parts_out[half], 16)

            store_parts(0)
            for half in range(2):
                sp.wait_ge(parts_out[half], 16 * 2 + 16)
            for half in range(2):
                store_parts(1 + half)
                load_q(0, 0, half)
                load_k(0, 0, half)
            store_parts(3)
            def max_rows_to(count, u, half):
                sp.wait_ge(ring_read, count)
                dst = qb[MROW:MROW + PARTS, u, half].rearrange("r e (a q) -> r (e a) q", q=P)
                sp.dma_start(dst, mT[:, half, :]).then_inc(m_in[half], 16)

            max_rows_to(FIRST_TURN + 1, 0, 0)
            for half in range(2):
                load_q(1, 1, half)
                load_k(1, 1, half)
            for half in range(2):
                sp.wait_ge(parts_out[half], 16 * 2 * B + 16)

            def sp_group(i, u, last):
                g = i * 2 + u
                pos = AT_RING_LAST if last and u == 1 else AT_RING
                base = i * (2 * RING_USES) + RING_USES * u + RING_FIRST + 1
                max_rows_to(base + pos["turned maxima", 1], u, 1)
                if not last:
                    sp.wait_ge(scores_done, i * (2 * NU) + NU * u + UNITS_OF[HT - 1][-1] + 1)
                    load_q(g + 2, u, 0)
                if not (last and u == 1):
                    max_rows_to(base + pos["turned maxima", 0], 1 - u, 0)
                if not last:
                    sp.wait_ge(scores_done, i * (2 * NU) + NU * u + UNITS_OF[2 * HT - 1][-1] + 1)
                    load_k(g + 2, u, 0)
                if not last:
                    sp.wait_ge(scores_done, i * (2 * NU) + NU * (u + 1))
                    load_q(g + 2, u, 1)
                    load_k(g + 2, u, 1)

            with sp.Fori(0, G // 2 - 1) as i:
                for u in range(2):
                    sp_group(i, u, False)
            for u in range(2):
                sp_group(G // 2 - 1, u, True)

            with sp.Fori(0, B) as b:
                for half in range(2):
                    sp.wait_ge(ffn_read, 2 * b + half + 3)
                    dst = o_v[:, bass.ds(b, 1), half * HT:(half + 1) * HT, :].rearrange("p o t d -> p (o t) d")
                    sp.dma_start(dst, xs[:, bass.ds(b * TILES + half * HT, HT), :]).then_inc(stored[half], 16)
            for half in range(2):
                sp.wait_ge(stored[half], 16 * B)

        @block.gpsimd
        def _(pool):
            pool.memset(vres[:].rearrange("p g (n c) -> p g n c", c=VC)[:, :, :, HD:VC], 1.0)
            pool.memset(vpad[:, :, :, :, VC:].rearrange("p u t e c -> p (u t e) c"), 0.0)
            pool.memset(mcut[:].bitcast(F32), 0.0).then_inc(zeroed, 1)

            with pool.Fori(0, B) as b:
                for half in range(2):
                    k = 2 * b + half
                    for qk in range(2):
                        pool.wait_ge(proj_read, 4 * k + 2 * qk + 2)
                        pool.tensor_tensor(prod[half][qk][:, 0], prod[half][qk][:, 0], prod[half][qk][:, 1],
                                           ALU.add).then_inc(rot_done, 1)
                    for qk in range(2):
                        pool.wait_ge(part0_done, 2 * k + qk + 1)
                        pool.tensor_tensor(rest[half][qk], prod[half][qk][:, 0], parts[:, half, qk, 0, :],
                                           ALU.subtract).then_inc(rest_done, 1)

            chain = [0]

            def done(ins):
                chain[0] += 1
                ins.then_inc(pool_step, 1)
                return chain[0]

            def cut_max(before, half, max_count):
                at0 = chain[0]

                def own(ins):
                    n = done(ins) - at0
                    pool.wait_ge(pool_step, before + n)
                pool.wait_ge((ring_read, max_joined)[half], max_count)
                m = negm[:, half, :]
                if half == 0:
                    src = mpart[:, 0, 0].rearrange("p e q -> p (e q)")
                else:
                    src = m
                n = HPG * HT
                pool.sem_inc(pool_gate)
                cut = [mcut[:, half, a * n:(a + 1) * n] for a in range(PARTS)]
                own(pool.tensor_copy(cut[0], src))
                own(pool.tensor_tensor(mrest[:, half, :], src, cut[0], ALU.subtract))
                pool.sem_inc(pool_gate)
                own(pool.tensor_copy(cut[1], mrest[:, half, :]))
                pool.tensor_tensor(cut[2], mrest[:, half, :], cut[1], ALU.subtract).then_inc(mcut_done, 1)

            def copy_v(g, u):
                pool.sem_inc(pool_gate)
                src = vres[:, g, :] if isinstance(g, int) else vres[:, bass.ds(g, 1), :].rearrange("p o f -> p (o f)")
                pool.tensor_copy(vpad[:, u, :, :, 0:VC].rearrange("p t e c -> p (t e) c"),
                                 src.rearrange("p (n c) -> p n c", c=VC)).then_inc(v_ready, 1)

            def diagonal(i, u, s):
                for n in UNITS_OF[s]:
                    _, _, heads = UNITS[n]
                    w = STEPS[s][3]
                    pool.wait_ge(exp_done, i * (2 * NU) + NU * u + n + 1)
                    pool.sem_inc(pool_gate)
                    at_slot = pr[:, (NU * u + n) % RING]
                    if heads == 2:
                        view, pat = at_slot[:, :, 0:P], [[0, 2], [1, P]]
                    else:
                        view = at_slot[:, :, 0:2 * w].rearrange("p a (c q) -> p a c q", c=2)[:, :, :, 0:P]
                        pat = [[0, 2], [0, 2], [1, P]]
                    pool.affine_select(out=view, in_=view, compare_op=ALU.is_ge, fill=0.0, base=0,
                                       pattern=pat, channel_multiplier=-1).then_inc(diag_done, 1)

            pool.wait_ge(v_read, 2 * B)
            copy_v(0, 0)
            cut_max(0, 0, M_END[0])
            for s in range(LEAD):
                diagonal(0, 0, s)
            pool.wait_ge(bias_ready, 1)

            def add_out_bias(g):
                n = B * TILES // G
                rows = xs[:, bass.ds(g * n, n), :]
                pool.tensor_tensor(rows, rows, bo[:].rearrange("p (o d) -> p o d", o=1).to_broadcast([P, n, D]), ALU.add)

            def pool_group(i, u, last):
                end = last and u == 1
                g = i * 2 + u
                cut_max(i * (2 * 6) + 3 + 6 * u, 1, i * 2 + u + 1)
                for s in range(LEAD, HT):
                    diagonal(i, u, s)
                if not end:
                    cut_max(i * (2 * 6) + 6 + 6 * u, 0, i * (2 * RING_USES) + RING_USES * u + RING_FIRST
                            + AT_RING["max", M_END[0] - 1] + 1)
                    pool.wait_ge(pv_done, i * (2 * NS) + NS * u + NS)
                    copy_v(g + 1, 1 - u)
                add_out_bias(g)
                if last:
                    for j in (range(0, 4), range(4, EARLY_HALVES))[u]:
                        b, hf = divmod(j, 2)
                        pool.tensor_copy(at_early[:, j, :].rearrange("p (t g c) -> p g t c", g=HG, t=HT),
                                         attn[:, b * HG:(b + 1) * HG, hf * HT:(hf + 1) * HT, :]).then_inc(at_early_done, 1)
                for s in range(2 * HT, NS):
                    diagonal(i, u, s)
                if not end:
                    nxt = (i, 1) if u == 0 else (i + 1, 0)
                    for s in range(LEAD):
                        diagonal(*nxt, s)

            with pool.Fori(0, G // 2 - 1) as i:
                for u in range(2):
                    pool_group(i, u, False)
            for u in range(2):
                pool_group(G // 2 - 1, u, True)

            with pool.Fori(0, B) as b:
                for half in range(2):
                    pool.wait_ge(yn_done, 2 * b + half + 1)
                    rows = xs[:, bass.ds(b * TILES + half * HT, HT), :]
                    pool.tensor_tensor(rows, rows, bf[:].rearrange("p (o d) -> p o d", o=1).to_broadcast([P, HT, D]),
                                       ALU.add).then_inc(ffn_bias_done, 1)

        @block.tensor
        def _(pe):
            pe.sem_inc(pv_done, NS)
            pe.sem_inc(oraw_done, 2)
            pe.sem_inc(ffn_read, 2)
            pe.wait_ge(consts_in, 16 * EARLY)

            def turn_tokens(b):
                for half in range(2):
                    pe.wait_ge(xn_done, 2 * b + half + 1)
                    for t in range(HT):
                        mm = pe.transpose(ps[:, 6 + half, t * P:(t + 1) * P], xn[:, half, t, :], ident[:])
                    mm.then_inc(xnT_turned, 1)

            def project(b, half):
                k = 2 * b + half
                pe.wait_ge(xnT_done, k + 1)
                for j in range(4):
                    if not (isinstance(k, int) and k == 0):
                        pe.wait_ge(proj_read, 4 * k + (j - 3))
                    pe.matmul(ps[:, 1 + j, :], wq[:, j, :], xnT[:, half, :],
                              start=True, stop=True).then_inc(proj_done, 1)
                if not (isinstance(k, int) and k < 2):
                    pe.wait_ge(v_read, k - 1)
                for t in range(HT):
                    mm = pe.matmul(ps[:, V_BANK[half], t * P:(t + 1) * P], xnT[:, half, t * P:(t + 1) * P], wq[:, 4, :],
                                   start=(t == 0), stop=True, skip_group_check=True)
                mm.then_inc(proj_done, 1)

            turn_tokens(0)
            for half in range(2):
                project(0, half)
            with pe.Fori(1, B) as b:
                turn_tokens(b)
                for half in range(2):
                    project(b, half)

            pe.wait_ge(late_in, 16 * LATE)
            pe.wait_ge(proj_read, 4 * 2 * B)

            def ring_bank(base, pos):
                if not (isinstance(base, int) and base + pos < NRING):
                    pe.wait_ge(ring_read, base + (pos - NRING + 1))
                return RING_BANK[pos % NRING]

            def max_scores(u, m, base, pos):
                half, qt, h0, heads, k0, w, diag, _ = MUNITS[m]
                bank = ring_bank(base, pos)
                for n in range(heads):
                    mm = pe.matmul(ps[:, bank, n * w:(n + 1) * w],
                                   qb[0:MROW, u, half, h0 + n, qt * P:(qt + 1) * P],
                                   kb[0:MROW, u, k0 // HALF, h0 + n, 0:w],
                                   start=(n == 0), stop=not diag, skip_group_check=True)
                if diag:
                    for n in range(heads):
                        mm = pe.matmul(ps[:, bank, (n + 1) * w - P:(n + 1) * w], identb[:], mask[:],
                                       start=False, stop=True, skip_group_check=True)
                mm.then_inc(ring_filled, 1)

            def wait_operands(i, u, half):
                pe.wait_ge(q_in[u][half], i * 48 + 48)
                pe.wait_ge(k_in[u][half], i * 48 + 48)

            def turn_max(base, pos, cuts, half):
                pe.wait_ge(mcut_done, cuts)
                bank = ring_bank(base, pos)
                pe.transpose(ps[:, bank, :].bitcast(BF16)[:, 0:P], mcut[:, half, :], identb[:]).then_inc(ring_filled, 1)

            def scores(i, u, n):
                s, h0, heads = UNITS[n]
                half, kt, c0, w, _ = STEPS[s]
                if not (isinstance(i, int) and i == 0 and u == 0 and n < 2):
                    pe.wait_ge(exp_done, i * (2 * NU) + NU * u + n - 1)
                bank = S_BANK[n % 2]
                per = heads // 2
                for m in range(heads):
                    col = (m % per) * w
                    mm = pe.matmul(ps[:, bank + m // per, col:col + w],
                                   kb[0:SROWS, u, kt // HT, h0 + m, (kt % HT) * P:(kt % HT + 1) * P],
                                   qb[0:SROWS, u, half, h0 + m, c0:HALF],
                                   start=(m % per == 0), stop=True, skip_group_check=True)
                mm.then_inc(scores_done, 1)

            def value_step(i, u, s):
                half, kt, c0, w, diag = STEPS[s]
                n = UNITS_OF[s][-1]
                if diag:
                    pe.wait_ge(diag_done, i * (2 * ND) + ND * u + DIAG.index(n) + 1)
                else:
                    pe.wait_ge(exp_done, i * (2 * NU) + NU * u + n + 1)
                if kt == 0:
                    pe.wait_ge(oraw_done, i * 4 + 2 * u + half + 2)
                if s == 0:
                    pe.wait_ge(v_ready, i * 2 + u + 1)
                for e in range(HPG):
                    if len(UNITS_OF[s]) == 2:
                        slot, src = (NU * u + UNITS_OF[s][e // 2]) % RING, (e % 2, 0)
                    else:
                        slot, src = (NU * u + n) % RING, (e // 2, (e % 2) * w)
                    mm = pe.matmul(ps[32 * e:32 * e + 32, PV_BANK, c0:HALF], vpad[:, u, kt, e, :],
                                   pr[:, slot, src[0], src[1]:src[1] + w],
                                   start=(kt == 0), stop=(s in HALF_END), skip_group_check=True)
                mm.then_inc(pv_done, 1)

            def turn_out(i, u, half, base, pos):
                pe.wait_ge(oraw_done, i * 4 + 2 * u + half + 3)
                bank = ring_bank(base, pos)
                for t in range(HT):
                    mm = pe.transpose(ps[:, bank, t * P:(t + 1) * P], oraw[:, half, t * P:(t + 1) * P], ident[:])
                mm.then_inc(ring_filled, 1)

            def turn_early(j, base, pos):
                pe.wait_ge(at_early_done, j + 1)
                bank = ring_bank(base, pos)
                for t in range(HT):
                    mm = pe.transpose(ps[:, bank, t * P:(t + 1) * P], at_early[:, j, t * P:(t + 1) * P], ident[:])
                mm.then_inc(ring_filled, 1)

            def project_early(j, base, pos, turned_pos):
                pe.wait_ge(ring_read, base + (turned_pos + 1))
                bank = ring_bank(base, pos)
                for t in range(HT):
                    mm = pe.matmul(ps[:, bank, t * P:(t + 1) * P], aT_early[:, j % 2, t * P:(t + 1) * P], wo[:],
                                   start=(t == 0), stop=True, skip_group_check=True)
                mm.then_inc(ring_filled, 1)

            pe.wait_ge(zeroed, 1)
            lead_units = [n for s in range(LEAD) for n in UNITS_OF[s]]
            for m in range(NM):
                if m == 0:
                    wait_operands(0, 0, 0)
                if m == M_END[0]:
                    wait_operands(0, 0, 1)
                if FIRST_POS[m] == RING_BANK.index(5):
                    pe.wait_ge(v_read, 2 * B)
                if m == FIRST_TURN:
                    turn_max(0, FIRST_TURN, 1, 0)
                    pe.matmul(ps[:, 0, 0:D], wr[:], dc[:], start=True, stop=False)
                    pe.matmul(ps[:, 0, 0:D], wi[:], dsn[:], start=False, stop=True)
                    pe.matmul(ps[:, 1, 0:D], wi[:], dc[:], start=True, stop=False)
                    pe.matmul(ps[:, 1, 0:D], wr[:], dns[:], start=False, stop=True).then_inc(ffn_a, 1)
                    pe.wait_ge(bias_done, 1)
                    pe.matmul(ps[:, 3, 0:D], bvw[:], wo[:], start=True, stop=True).then_inc(bias_row, 1)
                if m == FFN_AT:
                    pe.wait_ge(ffn_a_out, 1)
                    pe.matmul(ps[:, 2, 0:D], a12[:, 0, :], dc[:], start=True, stop=False)
                    pe.matmul(ps[:, 2, 0:D], a12[:, 1, :], dns[:], start=False, stop=True).then_inc(ffn_m, 1)
                if m == NM - 2 * len(lead_units):
                    pe.wait_ge(ffn_m_out, 1)
                    pe.wait_ge(bias_ready, 1)
                    pe.wait_ge(m_in[0], 16)
                if m >= NM - 2 * len(lead_units) and (NM - m) % 2 == 0:
                    scores(0, 0, lead_units[len(lead_units) - (NM - m) // 2])
                max_scores(0, m, 0, FIRST_POS[m])

            def pe_group(i, u, last):
                end = last and u == 1
                nxt = (i, 1) if u == 0 else (i + 1, 0)
                pos = AT_RING_LAST if end else AT_RING
                base = i * (2 * RING_USES) + RING_USES * u + RING_FIRST
                for s in range(NS):
                    a = s + LEAD
                    if a < NS:
                        units = [(i, u, n) for n in UNITS_OF[a]]
                    elif not end:
                        units = [(*nxt, n) for n in UNITS_OF[a - NS]]
                    else:
                        units = []
                    maxima = [] if end else list(range(M_AT[s], M_AT[s + 1]))

                    def some_maxima(count):
                        for m in maxima[:count]:
                            if m == 0:
                                wait_operands(*nxt, 0)
                            if m == M_END[0]:
                                wait_operands(*nxt, 1)
                            max_scores(1 - u, m, base, pos["max", m])
                        del maxima[:count]

                    if s in HALF_END:
                        some_maxima(M_PLAN[s][0])
                        value_step(i, u, s)
                    for k, n in enumerate(units):
                        some_maxima(M_PLAN[s][k + (s in HALF_END)])
                        if a == HT and k == 0:
                            pe.wait_ge(m_in[1], i * 32 + 16 * u + 32)
                        if a == NS and k == 0:
                            pe.wait_ge(m_in[0], i * 32 + 16 * u + 32)
                        scores(*n)
                    if s not in HALF_END:
                        some_maxima(M_PLAN[s][len(units)])
                        value_step(i, u, s)
                    some_maxima(M_PLAN[s][-1])
                    if end and s < EARLY_HALVES:
                        turn_early(s, base, pos["turned attention", s])
                    if end and 0 <= s - 1 < EARLY_HALVES:
                        project_early(s - 1, base, pos["projection", s - 1], pos["turned attention", s - 1])
                    if s == 0:
                        turn_max(base, pos["turned maxima", 1], i * 4 + 2 * u + 2, 1)
                    if s == A_T0:
                        turn_out(i, u, 0, base, pos["turned outputs", 0])
                    if s == M_T0 and not end:
                        turn_max(base, pos["turned maxima", 0], i * 4 + 2 * u + 3, 0)
                    if s == NS - 1:
                        turn_out(i, u, 1, base, pos["turned outputs", 1])

            with pe.Fori(0, G // 2 - 1) as i:
                for u in range(2):
                    pe_group(i, u, False)
            for u in range(2):
                pe_group(G // 2 - 1, u, True)

            def turn_outputs():
                for half in range(2):
                    pe.wait_ge(at_done, half + 1)
                    for t in range(HT):
                        mm = pe.transpose(ps[:, half, t * P:(t + 1) * P], at[half][:, t * P:(t + 1) * P], ident[:])
                    mm.then_inc(a_turned, 1)

            def project_out():
                for half in range(2):
                    pe.wait_ge(aT_done, half + 1)
                    for t in range(HT):
                        mm = pe.matmul(ps[:, 2 + half, t * P:(t + 1) * P], aT[half][:, t * P:(t + 1) * P], wo[:],
                                       start=(t == 0), stop=True, skip_group_check=True)
                    mm.then_inc(out_proj_done, 1)

            def turn_normed(b):
                for half in range(2):
                    pe.wait_ge(yn_done, 2 * b + half + 1)
                    for t in range(HT):
                        mm = pe.transpose(ps[:, 4 + half, t * P:(t + 1) * P], yn[half][:, t * P:(t + 1) * P], ident[:])
                    mm.then_inc(y_turned, 1)

            def spectral(b):
                for half in range(2):
                    pe.wait_ge(ynT_done, 2 * b + half + 1)
                    pe.wait_ge(ffn_read, 2 * b + half + 1)
                    for t in range(HT):
                        mm = pe.matmul(ps[:, 6 + half, t * P:(t + 1) * P], ynT[half][:, t * P:(t + 1) * P], mffn[:],
                                       start=(t == 0), stop=True, skip_group_check=True)
                    mm.then_inc(ffn_done, 1)

            pe.wait_ge(exp_done, NU * G)
            turn_outputs()
            project_out()
            with pe.Fori(0, B) as b:
                turn_normed(b)
                spectral(b)

        @block.scalar
        def _(act):
            def root(b):
                act.wait_ge(var_done, b + 1)
                act.activation(rstd[:], rstd[:], ACT.Sqrt).then_inc(std_done, 1)

            def tokens_out(b, half):
                act.wait_ge(xnT_turned, 2 * b + half + 1)
                act.copy(xnT[:, half, :], ps[:, 6 + half, :]).then_inc(xnT_done, 1)

            def values_out(b, half):
                act.wait_ge(proj_done, 5 * (2 * b + half) + 5)
                act.sem_inc(act_gate)
                for t in range(HT):
                    dst = vres[:, bass.ds(b * HG, HG), :].rearrange("p g (t e c) -> p g t e c", e=HPG, c=VC)[
                        :, :, half * HT + t, :, 0:HD]
                    ins = act.copy(dst, ps[:, V_BANK[half], t * P:(t + 1) * P].rearrange("p (g e c) -> p g e c", e=HPG, c=HD))
                ins.then_inc(v_read, 1)

            def first_parts(b, half):
                act.wait_ge(parts_out[half], b * (16 * 2) + 16)
                for qk in range(2):
                    act.wait_ge(rot_done, 4 * b + 2 * half + qk + 1)
                    act.copy(parts[:, half, qk, 0, :], prod[half][qk][:, 0]).then_inc(part0_done, 1)

            def second_parts(b, half):
                for qk in range(2):
                    act.wait_ge(rest_done, 4 * b + 2 * half + qk + 1)
                    act.copy(parts[:, half, qk, 1, :], rest[half][qk]).then_inc(part1_done, 1)

            def batch_out(b, last):
                values_out(b, 0)
                first_parts(b, 0)
                if not last:
                    root(b + 1)
                second_parts(b, 0)
                if not last:
                    tokens_out(b + 1, 0)
                    tokens_out(b + 1, 1)
                values_out(b, 1)
                first_parts(b, 1)
                second_parts(b, 1)

            def bring_table(function):
                act.activation(table_probe[:], vpad[:, 0, 0, 0, VC:VC + 1], function)

            act.wait_ge(zeroed, 1)
            bring_table(ACT.Sqrt)
            root(0)
            for half in range(2):
                tokens_out(0, half)
            with act.Fori(0, B - 1) as b:
                batch_out(b, False)
            batch_out(B - 1, True)
            bring_table(ACT.Exp)

            act.wait_ge(late_in, 16 * LATE)
            act.activation(bvw[:], ident[:], ACT.Identity, bias=bv[:, 0:1], scale=0.0).then_inc(bias_done, 1)
            act.wait_ge(ffn_a, 1)
            act.activation(a12[:], ps[:, 0:2, 0:D], ACT.Copy, scale=1.0 / D).then_inc(ffn_a_out, 1)
            act.wait_ge(ffn_m, 1)
            act.copy(mffn[:], ps[:, 2, 0:D]).then_inc(ffn_m_out, 1)

            def exp(i, u, n):
                s, _, heads = UNITS[n]
                w = STEPS[s][3]
                act.wait_ge(scores_done, i * (2 * NU) + NU * u + n + 1)
                behind = NU * u + n - RING
                if isinstance(i, int) and 2 * NU * i + behind < 0:
                    pass
                else:
                    step = NS * (behind // NU) + UNITS[behind % NU][0] + 1
                    act.wait_ge(pv_done, i * (2 * NS) + NS + step)
                wide = w * heads // 2
                act.activation(pr[:, (NU * u + n) % RING, :, 0:wide], ps[:, S_BANK[n % 2]:S_BANK[n % 2] + 2, 0:wide],
                               ACT.Exp, scale=SCALE).then_inc(exp_done, 1)

            for s in range(LEAD):
                for n in UNITS_OF[s]:
                    exp(0, 0, n)

            def act_group(i, u, last):
                end = last and u == 1
                nxt = (i, 1) if u == 0 else (i + 1, 0)
                for s in range(NS):
                    if end and s == NS - 1:
                        bring_table(ACT.Sqrt)
                        act.wait_ge(var3_done, 1)
                        act.activation(rs3[:, 0:(B - 1) * TILES], rs3[:, 0:(B - 1) * TILES],
                                       ACT.Sqrt).then_inc(std3_done, 1)
                    if s in HALF_END:
                        half = HALF_END.index(s)
                        act.wait_ge(pv_done, i * (2 * NS) + NS + NS * u + s + 1)
                        act.copy(oraw[:, half, :], ps[:, PV_BANK, :]).then_inc(oraw_done, 1)
                    a = s + LEAD
                    if a < NS:
                        for n in UNITS_OF[a]:
                            exp(i, u, n)
                    elif not end:
                        for n in UNITS_OF[a - NS]:
                            exp(*nxt, n)

            with act.Fori(0, G // 2 - 1) as i:
                for u in range(2):
                    act_group(i, u, False)
            for u in range(2):
                act_group(G // 2 - 1, u, True)

            act.wait_ge(ring_read, RING_FIRST + RING_USES * (G - 1) + len(AT_RING_LAST))
            for half in range(2):
                src = attn[:, (B - 1) * HG:, half * HT:(half + 1) * HT, :]
                act.copy(at[half].rearrange("p (t g c) -> p g t c", g=HG, t=HT), src).then_inc(at_done, 1)
            for half in range(2):
                act.wait_ge(a_turned, half + 1)
                act.copy(aT[half], ps[:, half, :]).then_inc(aT_done, 1)

            def normed_out(b):
                for half in range(2):
                    act.wait_ge(y_turned, 2 * b + half + 1)
                    act.copy(ynT[half], ps[:, 4 + half, :]).then_inc(ynT_done, 1)

            normed_out(0)
            act.wait_ge(var3_done, 2)
            act.activation(rs3[:, (B - 1) * TILES:], rs3[:, (B - 1) * TILES:], ACT.Sqrt).then_inc(std3_done, 1)
            with act.Fori(1, B) as b:
                normed_out(b)

        @block.vector
        def _(dve):
            def own(ins, count):
                ins.then_inc(dve_step, 1)
                dve.wait_ge(dve_step, count)

            def stats(b):
                dve.wait_ge(x_in, 16 * b + 16)
                dve.sem_inc(dve_gate)
                for t in range(TILES):
                    ins = dve.bn_stats(st[:, t, :], xs[:, bass.ds(b * TILES + t, 1), :].rearrange("p o d -> p (o d)"))
                own(ins, 3 * b + 1)
                dve.sem_inc(dve_gate)
                for t in range(TILES):
                    ins = dve.bn_aggr(mv[:, t, :], st[:, t, :])
                own(ins, 3 * b + 2)
                dve.tensor_scalar(rstd[:], mv[:, :, 1], EPS, None, ALU.add).then_inc(var_done, 1)

            def norm(b):
                dve.wait_ge(std_done, b + 1)
                own(dve.reciprocal(rstd[:], rstd[:]), 3 * b + 3)
                for half in range(2):
                    for t in range(HT):
                        j = half * HT + t
                        ins = dve.tensor_scalar(xn[:, half, t, :],
                                                xs[:, bass.ds(b * TILES + j, 1), :].rearrange("p o d -> p (o d)"),
                                                mv[:, j, 0:1], rstd[:, j:j + 1], ALU.subtract, ALU.mult)
                    ins.then_inc(xn_done, 1)

            def rotate(b, half):
                k = 2 * b + half
                for j in range(4):
                    dve.wait_ge(proj_done, 5 * k + j + 1)
                    dve.scalar_tensor_tensor(out=prod[half][j // 2][:, j % 2], in0=ps[:, 1 + j, :],
                                             scalar=bq[:, j:j + 1],
                                             in1=(tc, ts)[j % 2][:, half * HALF:(half + 1) * HALF],
                                             op0=ALU.add, op1=ALU.mult).then_inc(proj_read, 1)

            def third_parts(b, half):
                for qk in range(2):
                    dve.wait_ge(part1_done, 4 * b + 2 * half + qk + 1)
                    dve.tensor_tensor(parts[:, half, qk, 2, :], rest[half][qk], parts[:, half, qk, 1, :],
                                      ALU.subtract).then_inc(part2_done, 1)

            stats(0)
            norm(0)
            dve.wait_ge(consts_in, 16 * EARLY)
            def batch(b, first, last):
                rotate(b, 0)
                if not last:
                    stats(b + 1)
                if not first:
                    third_parts(b - 1, 1)
                if not last:
                    norm(b + 1)
                rotate(b, 1)
                third_parts(b, 0)

            batch(0, True, False)
            with dve.Fori(1, B - 1) as b:
                batch(b, False, False)
            batch(B - 1, False, True)
            n1 = 3 * B

            def take_max(m, base, pos):
                half, qt, h0, heads, _, w, _, which = MUNITS[m]
                dve.wait_ge(ring_filled, base + (pos + 1))
                dve.tensor_reduce(mpart[:, half, which, h0:h0 + heads, qt],
                                  ps[:, RING_BANK[pos % NRING], 0:heads * w].rearrange("p (e k) -> p e k", e=heads),
                                  AX_X, ALU.max, negate=True).then_inc(ring_read, 1)
                if m == NM - 1:
                    dve.wait_ge(ring_read, base + (pos + 1))
                    dve.tensor_tensor(negm[:, 1, :], mpart[:, 1, 0].rearrange("p e q -> p (e q)"),
                                      mpart[:, 1, 1].rearrange("p e q -> p (e q)"), ALU.min).then_inc(max_joined, 1)

            def max_row_out(base, pos, half, rows):
                dve.wait_ge(ring_filled, base + (pos + 1))
                if rows is not None:
                    dve.wait_ge(m_in[half], rows)
                n = PARTS * HPG * HT
                dve.tensor_copy(mT[:, half, :],
                                ps[0:n, RING_BANK[pos % NRING], :].bitcast(BF16)[:, 0:P]).then_inc(ring_read, 1)

            def outputs(i, u, half, base, pos, own_count):
                dve.wait_ge(ring_filled, base + (pos + 1))
                o = ps[:, RING_BANK[pos % NRING], :].rearrange("p (t e c) -> p t e c", t=HT, c=32)
                own(dve.reciprocal(rden[:, half], o[:, :, :, HD]), own_count)
                g = i * 2 + u
                dst = attn[:, bass.ds(g, 1), half * HT:(half + 1) * HT, :] if not isinstance(g, int) else \
                    attn[:, g:g + 1, half * HT:(half + 1) * HT, :]
                dst = dst.rearrange("p o t (e c) -> p (o t) e c", c=HD)
                dve.tensor_tensor(dst, o[:, :, :, 0:HD],
                                  rden[:, half].rearrange("p t (e o) -> p t e o", o=1).to_broadcast([P, HT, HPG, HD]),
                                  ALU.mult).then_inc(ring_read, 1)

            for m in range(NM):
                if m == M_END[0]:
                    third_parts(B - 1, 1)
                if m == FIRST_TURN:
                    max_row_out(0, FIRST_TURN, 0, None)
                if m == FFN_AT:
                    dve.wait_ge(bias_row, 1)
                    dve.tensor_tensor(bo[:], bo[:], ps[:, 3, 0:D], ALU.add).then_inc(bias_ready, 1)
                take_max(m, 0, FIRST_POS[m])

            def turned_early(j, base, pos):
                dve.wait_ge(ring_filled, base + (pos + 1))
                dve.tensor_copy(aT_early[:, j % 2, :], ps[:, RING_BANK[pos % NRING], :]).then_inc(ring_read, 1)

            def half_stats(b, half):
                for t in range(half * HT, (half + 1) * HT):
                    ins = dve.bn_stats(st3[:, t, :], xs[:, b * TILES + t, :])
                return ins

            def variances(b, ins, count):
                ins.then_inc(stats_step, 1)
                dve.wait_ge(stats_step, count + 1)
                for t in range(TILES):
                    ins = dve.bn_aggr(mv3[:, t, :], st3[:, t, :])
                ins.then_inc(stats_step, 1)
                dve.wait_ge(stats_step, count + 2)
                dve.tensor_copy(mean3[:, b * TILES:(b + 1) * TILES], mv3[:, :, 0])
                return dve.tensor_scalar(rs3[:, b * TILES:(b + 1) * TILES], mv3[:, :, 1], EPS, None, ALU.add)

            def residual_early(j, base, pos):
                b, half = divmod(j, 2)
                dve.wait_ge(ring_filled, base + (pos + 1))
                rows = xs[:, b * TILES + half * HT:b * TILES + (half + 1) * HT, :]
                dve.tensor_tensor(rows, rows, ps[:, RING_BANK[pos % NRING], :].rearrange("p (t d) -> p t d", d=D),
                                  ALU.add).then_inc(ring_read, 1)
                dve.wait_ge(ring_read, base + (pos + 1))
                ins = half_stats(b, half)
                if half == 1:
                    ins = variances(b, ins, 2 * b)
                    if b == B - 2:
                        ins.then_inc(var3_done, 1)

            def reciprocal3(b0, b1, roots, count):
                dve.wait_ge(std3_done, roots)
                r3 = rs3[:, b0 * TILES:b1 * TILES]
                dve.reciprocal(r3, r3).then_inc(stats_step, 1)
                dve.wait_ge(stats_step, count)

            def norm3(b):
                for half in range(2):
                    if not (isinstance(b, int) and b == 0):
                        dve.wait_ge(y_turned, 2 * b + half - 1)
                    for t in range(HT):
                        j = b * TILES + half * HT + t
                        ins = dve.tensor_scalar(yn[half][:, t * P:(t + 1) * P],
                                                xs[:, bass.ds(j, 1), :].rearrange("p o d -> p (o d)"),
                                                mean3[:, bass.ds(j, 1)], rs3[:, bass.ds(j, 1)],
                                                ALU.subtract, ALU.mult)
                    ins.then_inc(yn_done, 1)

            def dve_group(i, u, last):
                end = last and u == 1
                pos = AT_RING_LAST if end else AT_RING
                base = i * (2 * RING_USES) + RING_USES * u + RING_FIRST
                for s in range(NS):
                    if not end:
                        for m in range(M_AT[s], M_AT[s + 1]):
                            take_max(m, base, pos["max", m])
                    if end and s < EARLY_HALVES:
                        turned_early(s, base, pos["turned attention", s])
                    if end and 0 <= s - 1 < EARLY_HALVES:
                        residual_early(s - 1, base, pos["projection", s - 1])
                    if s == 0:
                        max_row_out(base, pos["turned maxima", 1], 1, i * 32 + 16 * u + 16)
                    if s == A_T0:
                        outputs(i, u, 0, base, pos["turned outputs", 0], i * 4 + n1 + 2 * u + 1)
                    if s == M_T0 and not end:
                        max_row_out(base, pos["turned maxima", 0], 0, i * 32 + 16 * u + 16)
                    if s == NS - 1:
                        outputs(i, u, 1, base, pos["turned outputs", 1], i * 4 + n1 + 2 * u + 2)

            with dve.Fori(0, G // 2 - 1) as i:
                for u in range(2):
                    dve_group(i, u, False)
            for u in range(2):
                dve_group(G // 2 - 1, u, True)

            def residual():
                b = B - 1
                for half in range(2):
                    dve.wait_ge(out_proj_done, half + 1)
                    rows = xs[:, b * TILES + half * HT:b * TILES + (half + 1) * HT, :]
                    dve.tensor_tensor(rows, rows, ps[:, 2 + half, :].rearrange("p (t d) -> p t d", d=D),
                                      ALU.add).then_inc(out_proj_read, 1)
                for half in range(2):
                    dve.wait_ge(out_proj_read, half + 1)
                    ins = half_stats(b, half)
                variances(b, ins, 2 * b + 1).then_inc(var3_done, 1)

            def finish(b):
                for half in range(2):
                    dve.wait_ge(ffn_bias_done, 2 * b + half + 1)
                    dve.wait_ge(ffn_done, 2 * b + half + 1)
                    rows = xs[:, bass.ds(b * TILES + half * HT, HT), :]
                    dve.tensor_tensor(rows, rows, ps[:, 6 + half, :].rearrange("p (t d) -> p t d", d=D),
                                      ALU.add).then_inc(ffn_read, 1)

            reciprocal3(0, B - 1, 1, 2 * (B - 1) + 1)
            norm3(0)
            residual()
            with dve.Fori(0, B - 2) as b:
                norm3(b + 1)
                finish(b)
            reciprocal3(B - 1, B, 2, 2 * B + 2)
            norm3(B - 1)
            finish(B - 2)
            finish(B - 1)


def kernel(**inputs):
    import numpy as np
    import concourse.bacc as bacc
    from concourse.bass_utils import run_bass_kernel_spmd as run

    x = np.ascontiguousarray(inputs["L0_attn_x"])
    w = np.asarray(inputs["L0_attn_qkv_w"])
    bias = np.asarray(inputs["L0_attn_qkv_b"])

    g, d, e = np.meshgrid(np.arange(HG), np.arange(HD), np.arange(HPG), indexing="ij")
    even = 2 * (d % (HD // 2)) + d // (HD // 2)
    odd = 2 * (d % (HD // 2)) + 1 - d // (HD // 2)
    head = (g * HPG + e) * HD
    straight, swapped = (head + even).reshape(-1), (head + odd).reshape(-1)
    cols = [straight, swapped, D + straight, D + swapped]
    w_qkv = np.ascontiguousarray(np.stack([w[:, c] for c in cols] + [w[:, 2 * D:]], axis=1))
    b_qk = np.ascontiguousarray(np.stack([bias[c] for c in cols], axis=1))

    f = (np.float32(1.0) / np.float32(10000.0) ** (np.arange(0, HD, 2, dtype=np.float32) / np.float32(HD))).astype(np.float32)
    angle = (np.arange(T, dtype=np.float32)[:, None] * f[None, :]).astype(np.float64)
    rope = np.concatenate([np.sin(angle), np.cos(angle)], axis=-1)
    sin, cos = rope[:, 0::2], rope[:, 1::2]
    dim = d.reshape(-1)
    rope_c = np.ascontiguousarray(cos[:, dim % 4].T.astype(np.float32))
    rope_s = np.ascontiguousarray((sin[:, dim % 4] * np.where(dim < 4, -1.0, 1.0)).T.astype(np.float32))
    k = np.arange(D)
    turn = 2 * np.pi * (k[:, None] * k[None, :] % D) / D
    dft_c, dft_s = np.cos(turn).astype(np.float32), np.sin(turn).astype(np.float32)
    eye = np.eye(P, dtype=np.float32)
    bf = mybir.dt.np(BF16)
    future = np.where(np.arange(P)[None, :] > np.arange(P)[:, None], NEG, 0.0).astype(bf)

    pad = np.zeros((SROWS - KROWS, 2 * 2 * HPG * HALF), bf)
    pad[MROW - KROWS:] = 1

    nc = bacc.Bacc("TRN2", target_bir_lowering=False, num_devices=1)
    arrays, args = {}, []
    for name, a in (("x", x), ("w_qkv", w_qkv), ("b_qk", b_qk), ("b_v", bias[2 * D:, None]),
                    ("w_out", inputs["L0_attn_out_w"]), ("b_out", np.asarray(inputs["L0_attn_out_b"])[None, :]),
                    ("w_re", inputs["L0_ffn_w_freq_real"]), ("w_im", inputs["L0_ffn_w_freq_imag"]),
                    ("b_ffn", np.asarray(inputs["L0_ffn_bias"])[None, :]),
                    ("rope_c", rope_c), ("rope_s", rope_s), ("dft_c", dft_c), ("dft_s", dft_s), ("dft_ns", -dft_s),
                    ("ident", eye), ("identb", eye.astype(bf)), ("mask", future), ("pad", pad)):
        a = np.ascontiguousarray(a)
        arrays[f"in_{name}"] = a
        args.append(nc.dram_tensor(f"in_{name}", a.shape, mybir.dt.from_np(a.dtype), kind="ExternalInput").ap())
    for name in ("q_scr", "k_scr"):
        args.append(nc.dram_tensor(name, (2, PARTS, B, HG, HD * HPG, HALF), BF16, kind="Internal").ap())
    args.append(nc.dram_tensor("out_0", (B, T, D), F32, kind="ExternalOutput").ap())
    build(nc, *args)
    r = run(nc, [arrays], core_ids=[0])
    return r.results[0]["out_0"]
```
